# Optimizing a Trainium2 kernel written in Bass

```python
import numpy as np
import jax
import jax.numpy as jnp

def _softmax(x, axis=-1):
    return jax.nn.softmax(x, axis=axis)

def _gelu(x):
    return jax.nn.gelu(x, approximate=True)

def _silu(x):
    return jax.nn.silu(x)

def _sigmoid(x):
    return jax.nn.sigmoid(x)

def _layernorm(x, axis=-1, eps=1e-05):
    m = jnp.mean(x, axis=axis, keepdims=True)
    v = jnp.var(x, axis=axis, keepdims=True)
    return (x - m) / jnp.sqrt(v + eps)

def _scatter_add(tgt, idx, src, axis=0):
    return tgt.at[idx].add(src)

def _segment_sum(src, seg, n):
    return jax.ops.segment_sum(src, seg, n)
kernel_name = 'mk_gnn_preln_d4_gnn_r32_5ce2f7'

def setup_inputs(seed: int=0):
    np.random.seed(seed)
    _w = jnp.asarray

    def _rec_inputs():
        import jax
        import jax.numpy as jnp
        _gk = jax.random.key(seed)
        x = -0.0006008 + 1.001 * jax.random.normal(jax.random.fold_in(_gk, 1), (50000, 256), jnp.float32)
        src = jax.random.randint(jax.random.fold_in(_gk, 2), (50000,), 0, 50000, jnp.int32)
        dst = jnp.minimum((50000 * jax.random.uniform(jax.random.fold_in(_gk, 3), (50000,)) ** 2.0).astype(jnp.int32), 49999)
        _o = jnp.argsort(dst, stable=True)
        src = src[_o]
        dst = dst[_o]
        edge_attr_2 = jax.random.uniform(jax.random.fold_in(_gk, 12), (50000, 2), jnp.float32, 0.0, 1)
        edge_weight = jax.random.uniform(jax.random.fold_in(_gk, 14), (50000,), jnp.float32, 0.0, 1)
        return (x, src, dst, edge_attr_2, edge_weight)
    x, src, dst, edge_attr_2, edge_weight = _rec_inputs()

    def _L0_gnn_setup():
        import jax, jax.numpy as jnp
        import numpy as np
        N_NODES = 10000
        N_EDGES = 10000
        D_IN = 256
        D_OUT = 256
        MAX_NORM = 0.95

        def _expmap0(u):
            un = jnp.linalg.norm(u, axis=-1, keepdims=True)
            un_c = jnp.maximum(un, 1e-15)
            return jnp.tanh(un_c) * u / un_c
        key = jax.random.key(seed)
        ks = jax.random.split(key, 7)
        x = jax.random.normal(ks[0], (N_NODES, D_IN), dtype=jnp.float32)
        edge_index = jax.random.randint(ks[1], (2, N_EDGES), 0, N_NODES, dtype=jnp.int64)
        W = jax.random.normal(ks[2], (D_OUT, D_IN), dtype=jnp.float32) * (1.0 / np.sqrt(D_IN))
        b = jax.random.normal(ks[3], (D_OUT,), dtype=jnp.float32) * 0.02
        mag_w = jax.random.normal(ks[4], (1, D_IN), dtype=jnp.float32) * 0.02
        mag_b = jax.random.normal(ks[5], (1,), dtype=jnp.float32) * 0.02
        attn_w = jax.random.normal(ks[6], (1, 2 * D_OUT), dtype=jnp.float32) * (1.0 / np.sqrt(2 * D_OUT))
        return {'x': x, 'edge_index': edge_index, 'W': W, 'b': b, 'mag_w': mag_w, 'mag_b': mag_b, 'attn_w': attn_w}
    _L0_gnn_all = _L0_gnn_setup()
    _L0_gnn_in = {k: v for k, v in _L0_gnn_all.items() if k in ('W', 'b', 'mag_w', 'mag_b', 'attn_w')}
    del _L0_gnn_all

    def _L1_gnn_setup():
        import jax, jax.numpy as jnp
        import numpy as np
        N_NODES = 3125
        N_EDGES = 100000
        D_IN = 256
        D_OUT = 256
        key = jax.random.key(seed)
        k1, k2, k3, k4, k5, k6 = jax.random.split(key, 6)
        x = jax.random.normal(k1, (N_NODES, D_IN), dtype=jnp.float32)
        edge_src = jax.random.randint(k2, (N_EDGES,), 0, N_NODES, dtype=jnp.int64)
        edge_dst = jax.random.randint(k3, (N_EDGES,), 0, N_NODES, dtype=jnp.int64)
        adj_vals = jax.random.uniform(k4, (N_EDGES,), dtype=jnp.float32)
        bound = 2.0 * np.sqrt(6.0 / (D_IN + D_OUT))
        w_nbr = jax.random.uniform(k5, (D_IN, D_OUT), dtype=jnp.float32, minval=-bound, maxval=bound)
        w_own = jax.random.uniform(k6, (D_IN, D_OUT), dtype=jnp.float32, minval=-bound, maxval=bound)
        bias = jnp.zeros((D_OUT,), dtype=jnp.float32)
        return {'x': x, 'edge_src': edge_src, 'edge_dst': edge_dst, 'adj_vals': adj_vals, 'w_nbr': w_nbr, 'w_own': w_own, 'bias': bias}
    _L1_gnn_all = _L1_gnn_setup()
    _L1_gnn_in = {k: v for k, v in _L1_gnn_all.items() if k in ('w_nbr', 'w_own', 'bias')}
    del _L1_gnn_all

    def _L2_gnn_setup():
        import jax, jax.numpy as jnp
        import numpy as np
        N_NODES = 10000
        N_EDGES = 10000
        D_IN = 256
        D_OUT = 256
        NEG_SLOPE = 0.2
        key = jax.random.key(seed)
        ks = jax.random.split(key, 8)
        feature = jax.random.normal(ks[0], (N_NODES, D_IN), dtype=jnp.float32)
        src = jax.random.randint(ks[1], (N_EDGES,), 0, N_NODES, dtype=jnp.int32)
        dst = jax.random.randint(ks[2], (N_EDGES,), 0, N_NODES, dtype=jnp.int32)
        s = 1.0 / np.sqrt(D_IN)
        W_s = jax.random.normal(ks[3], (D_OUT, D_IN), dtype=jnp.float32) * s
        W_t = jax.random.normal(ks[4], (D_OUT, D_IN), dtype=jnp.float32) * s
        W_attn = jax.random.normal(ks[5], (1, D_OUT), dtype=jnp.float32) * (1.0 / np.sqrt(D_OUT))
        W_fc = jax.random.normal(ks[6], (D_OUT, D_IN), dtype=jnp.float32) * s
        b_fc = jnp.zeros((D_OUT,), dtype=jnp.float32)
        return {'feature': feature, 'src': src, 'dst': dst, 'W_s': W_s, 'W_t': W_t, 'W_attn': W_attn, 'W_fc': W_fc, 'b_fc': b_fc}
    _L2_gnn_all = _L2_gnn_setup()
    _L2_gnn_in = {k: v for k, v in _L2_gnn_all.items() if k in ('W_s', 'W_t', 'W_attn', 'W_fc', 'b_fc')}
    del _L2_gnn_all

    def _L3_gnn_setup():
        import jax, jax.numpy as jnp
        import numpy as np
        N_NODES = 3125
        N_EDGES = 50000
        IN_FEATS = 256
        OUT_FEATS = 64
        NUM_HEADS = 4
        key = jax.random.key(seed)
        k_h, k_adj, k_dir, k_wf, k_wr, k_af = jax.random.split(key, 6)
        h = jax.random.normal(k_h, (N_NODES, IN_FEATS), dtype=jnp.float32)
        adj = jax.random.randint(k_adj, (2, N_EDGES), 0, N_NODES, dtype=jnp.int64)
        bit = jax.random.randint(k_dir, (N_EDGES,), 0, 2).astype(jnp.float32)
        direction = jnp.stack([bit, 1.0 - bit], axis=1)
        s_w = float(np.sqrt(6.0 / (IN_FEATS + OUT_FEATS)))
        s_a = float(np.sqrt(6.0 / (NUM_HEADS + OUT_FEATS)))
        W_forward = jax.random.uniform(k_wf, (OUT_FEATS, IN_FEATS), jnp.float32, -s_w, s_w)
        W_reverse = jax.random.uniform(k_wr, (OUT_FEATS, IN_FEATS), jnp.float32, -s_w, s_w)
        attn_forward = jax.random.uniform(k_af, (1, NUM_HEADS, OUT_FEATS), jnp.float32, -s_a, s_a)
        return {'h': h, 'adj': adj, 'direction': direction, 'W_forward': W_forward, 'W_reverse': W_reverse, 'attn_forward': attn_forward}
    _L3_gnn_all = _L3_gnn_setup()
    _L3_gnn_in = {k: v for k, v in _L3_gnn_all.items() if k in ('W_forward', 'W_reverse', 'attn_forward')}
    del _L3_gnn_all
    return {'x': x, 'src': src, 'dst': dst, 'edge_attr_2': edge_attr_2, 'edge_weight': edge_weight, 'L0_gnn_W': _L0_gnn_in['W'], 'L0_gnn_b': _L0_gnn_in['b'], 'L0_gnn_mag_w': _L0_gnn_in['mag_w'], 'L0_gnn_mag_b': _L0_gnn_in['mag_b'], 'L0_gnn_attn_w': _L0_gnn_in['attn_w'], 'L1_gnn_w_nbr': _L1_gnn_in['w_nbr'], 'L1_gnn_w_own': _L1_gnn_in['w_own'], 'L1_gnn_bias': _L1_gnn_in['bias'], 'L2_gnn_W_s': _L2_gnn_in['W_s'], 'L2_gnn_W_t': _L2_gnn_in['W_t'], 'L2_gnn_W_attn': _L2_gnn_in['W_attn'], 'L2_gnn_W_fc': _L2_gnn_in['W_fc'], 'L2_gnn_b_fc': _L2_gnn_in['b_fc'], 'L3_gnn_W_forward': _L3_gnn_in['W_forward'], 'L3_gnn_W_reverse': _L3_gnn_in['W_reverse'], 'L3_gnn_attn_forward': _L3_gnn_in['attn_forward']}

def reference(x, src, dst, edge_attr_2, edge_weight, L0_gnn_W, L0_gnn_b, L0_gnn_mag_w, L0_gnn_mag_b, L0_gnn_attn_w, L1_gnn_w_nbr, L1_gnn_w_own, L1_gnn_bias, L2_gnn_W_s, L2_gnn_W_t, L2_gnn_W_attn, L2_gnn_W_fc, L2_gnn_b_fc, L3_gnn_W_forward, L3_gnn_W_reverse, L3_gnn_attn_forward):
    import jax
    import jax.numpy as jnp

    def _L0_gnn_ref(x, edge_index, W, b, mag_w, mag_b, attn_w):
        import jax, jax.numpy as jnp
        import numpy as np
        N_NODES = 10000
        N_EDGES = 10000
        D_IN = 256
        D_OUT = 256
        MAX_NORM = 0.95

        def _expmap0(u):
            un = jnp.linalg.norm(u, axis=-1, keepdims=True)
            un_c = jnp.maximum(un, 1e-15)
            return jnp.tanh(un_c) * u / un_c
        N = x.shape[0]
        F_out = W.shape[0]
        h_raw = x @ W.T + b
        h_dir = h_raw / jnp.maximum(jnp.linalg.norm(h_raw, axis=-1, keepdims=True), 1e-12)
        h_mag = jax.nn.sigmoid(x @ mag_w.T + mag_b) * 1.5
        h = h_dir * h_mag
        src, tgt = (edge_index[0], edge_index[1])
        h_src = h[src]
        h_tgt = h[tgt]
        a_s, a_t = (attn_w[0, :F_out], attn_w[0, F_out:])
        scores = h_src @ a_s + h_tgt @ a_t
        mx = jnp.maximum(jax.ops.segment_max(scores, tgt, num_segments=N), -1000000000.0)
        ex = jnp.exp(scores - mx[tgt])
        se = jax.ops.segment_sum(ex, tgt, num_segments=N)
        attn_weights = ex / (se[tgt] + 1e-10)
        agg = jax.ops.segment_sum(h_src * attn_weights[:, None], tgt, num_segments=N)
        h_combined = h + agg
        h_poincare = _expmap0(h_combined)
        norms = jnp.linalg.norm(h_poincare, axis=1, keepdims=True)
        return jnp.where(norms > MAX_NORM, h_poincare * (MAX_NORM / (norms + 1e-08)), h_poincare)

    def _L1_gnn_ref(x, edge_src, edge_dst, adj_vals, w_nbr, w_own, bias):
        import jax, jax.numpy as jnp
        import numpy as np
        N_NODES = 3125
        N_EDGES = 100000
        D_IN = 256
        D_OUT = 256
        h = x @ w_nbr
        msgs = adj_vals[:, None] * h[edge_src]
        agg = jax.ops.segment_sum(msgs, edge_dst, num_segments=x.shape[0])
        return agg + x @ w_own + bias

    def _L2_gnn_ref(feature, src, dst, W_s, W_t, W_attn, W_fc, b_fc):
        import jax, jax.numpy as jnp
        import numpy as np
        N_NODES = 10000
        N_EDGES = 10000
        D_IN = 256
        D_OUT = 256
        NEG_SLOPE = 0.2
        n = feature.shape[0]
        proj_s = feature @ W_s.T
        proj_t = feature @ W_t.T
        z = proj_s[src] + proj_t[dst]
        z = jnp.where(z >= 0, z, NEG_SLOPE * z)
        e = (z @ W_attn.T)[:, 0]
        m = jax.ops.segment_max(e, src, num_segments=n)
        m = jnp.where(jnp.isfinite(m), m, 0.0)
        e_exp = jnp.exp(e - m[src])
        denom = jax.ops.segment_sum(e_exp, src, num_segments=n)
        alpha = e_exp / denom[src]
        msg = feature[src] * alpha[:, None]
        agg = jax.ops.segment_sum(msg, dst, num_segments=n)
        return agg @ W_fc.T + b_fc

    def _L3_gnn_ref(h, adj, direction, W_forward, W_reverse, attn_forward):
        import jax, jax.numpy as jnp
        import numpy as np
        N_NODES = 3125
        N_EDGES = 50000
        IN_FEATS = 256
        OUT_FEATS = 64
        NUM_HEADS = 4
        N = h.shape[0]
        H = attn_forward.shape[1]
        h_fwd = h @ W_forward.T
        h_rev = h @ W_reverse.T
        src, dst = (adj[0], adj[1])
        messages = h_fwd[src] * direction[:, 0:1] + h_rev[src] * direction[:, 1:2]
        scores = jnp.einsum('ef,hf->eh', messages, attn_forward[0])
        scores = jax.nn.leaky_relu(scores, negative_slope=0.2)
        exp_scores = jnp.exp(scores - scores.max(axis=0, keepdims=True))
        sum_exp = jax.ops.segment_sum(exp_scores, dst, num_segments=N)
        norm = exp_scores / (sum_exp[dst] + 1e-10)
        outs = [jax.ops.segment_sum(messages * norm[:, hd:hd + 1], dst, num_segments=N) for hd in range(H)]
        out = jnp.stack(outs, axis=1)
        return out.reshape(N, -1)
    edge_index = jnp.stack([src, dst])
    h = jnp.maximum(_layernorm(x, axis=-1), 0.0)
    x = x + _L0_gnn_ref(h, edge_index, L0_gnn_W, L0_gnn_b, L0_gnn_mag_w, L0_gnn_mag_b, L0_gnn_attn_w)
    h = jnp.maximum(_layernorm(x, axis=-1), 0.0)
    x = x + _L1_gnn_ref(h, src, dst, edge_weight, L1_gnn_w_nbr, L1_gnn_w_own, L1_gnn_bias)
    h = jnp.maximum(_layernorm(x, axis=-1), 0.0)
    x = x + _L2_gnn_ref(h, src, dst, L2_gnn_W_s, L2_gnn_W_t, L2_gnn_W_attn, L2_gnn_W_fc, L2_gnn_b_fc)
    h = jnp.maximum(_layernorm(x, axis=-1), 0.0)
    x = x + _L3_gnn_ref(h, edge_index, edge_attr_2, L3_gnn_W_forward, L3_gnn_W_reverse, L3_gnn_attn_forward)
    return x

_drawn_inputs = setup_inputs


def setup_inputs(seed=0):
    import zlib

    import numpy as np

    out = dict(_drawn_inputs(seed))
    spreads = {'L1_gnn_bias': (0.0, 0.1), 'L2_gnn_b_fc': (0.0, 0.1)}
    factors = {'L0_gnn_b': 44.899, 'L0_gnn_mag_w': 85.48, 'L0_gnn_attn_w': 200.0, 'L2_gnn_W_s': 63.496}
    for name, (base, spread) in spreads.items():
        noise = np.random.default_rng([zlib.crc32(name.encode()), seed]).standard_normal(out[name].shape)
        drawn = base * np.exp(spread * noise) if base else spread * noise
        out[name] = jnp.asarray(drawn.astype(out[name].dtype))
    for name, factor in factors.items():
        out[name] = (out[name] * factor).astype(out[name].dtype)
    return out
```

```python
from contextlib import ExitStack

import concourse.bass as bass
from concourse import mybir

ALU = mybir.AluOpType
ACT = mybir.ActivationFunctionType
AX = mybir.AxisListType
F32 = mybir.dt.float32
BF16 = mybir.dt.bfloat16
I32 = mybir.dt.int32

P = 128
U = 8
D = 256
AGG_W = 260
FAR = 1e30
SKIP = 1 << 20


class Phase:

    def __init__(self, nc, name):
        self.nc, self.name, self.sems, self.ctx = nc, name, [], ExitStack()

    def sb(self, name, shape, dt=F32):
        return self.ctx.enter_context(self.nc.sbuf_tensor(f"{self.name}_{name}", shape, dt))

    def ps(self, name, shape, dt=F32):
        return self.ctx.enter_context(self.nc.psum_tensor(f"{self.name}_{name}", shape, dt))

    def sem(self, name):
        self.sems.append(self.nc.alloc_semaphore(f"{self.name}_{name}"))
        return self.sems[-1]

    def sem_per_slot(self, name, n=U):
        return [self.sem(f"{name}{j}") for j in range(n)]

    def close(self):
        self.nc.clear_and_free_semaphores(self.sems)
        self.nc.all_engine_barrier()
        self.ctx.close()


def peeled(engine, count, body):
    body(0, True)
    if count > 1:
        with engine.Fori(1, count) as i:
            body(i, False)


class Chain:

    def __init__(self, engine, sem):
        self.engine, self.sem, self.n = engine, sem, 0

    def __call__(self, instruction):
        self.n += 1
        instruction.then_inc(self.sem, 1)
        self.engine.wait_ge(self.sem, self.n)


def columns(t, c, n=1):
    return t[:, bass.ds(c, n)]


def constants(nc, k):
    ph = Phase(nc, "const")
    filled, s_done = ph.sem("filled"), ph.sem("done")
    with nc.Block() as block:
        @block.gpsimd
        def _(pool):
            nc.gpsimd.memset(k.ones[:], 1.0).then_inc(filled, 1)
            nc.gpsimd.iota(k.ramp_i[:], pattern=[[1, k.TC]], base=0, channel_multiplier=0).then_inc(filled, 1)
            pool.wait_ge(filled, 2)
            nc.gpsimd.affine_select(out=k.ident[:], in_=k.ones[:], compare_op=ALU.is_equal, fill=0.0, base=0,
                                    pattern=[[-1, P]], channel_multiplier=1).then_inc(s_done, 1)
            nc.gpsimd.affine_select(out=k.before[:], in_=k.ones[:], compare_op=ALU.is_gt, fill=0.0, base=0,
                                    pattern=[[1, P]], channel_multiplier=-1).then_inc(s_done, 1)

        @block.vector
        def _(dve):
            nc.vector.memset(k.pos_i[:], 0).then_inc(s_done, 1)
            dve.wait_ge(filled, 2)
            nc.vector.tensor_copy(k.ramp[:], k.ramp_i[:]).then_inc(s_done, 1)
            dve.wait_ge(s_done, 4)
            nc.vector.tensor_copy(k.ident_bf[:], k.ident[:]).then_inc(s_done, 1)
    ph.close()


def load_edges(nc, k, a):
    ph = Phase(nc, "load")
    E, TC, B = k.E, k.TC, k.TC // P
    raw_i = [ph.sb(f"raw_i{n}", [P, B, P], I32) for n in range(2)]
    raw = [ph.sb(f"raw{n}", [P, B, P]) for n in range(3)]
    pair = ph.sb("pair", [P, B, P, 2])
    part = [ph.sb(f"part{n}", [P, B, P]) for n in range(2)]
    turned = [ph.ps(f"turned{n}", [P, B * P]) for n in range(5)]
    preset, landed, cast, turn, s_done = (ph.sem(n) for n in ("preset", "landed", "cast", "turn", "done"))
    full, rest = E // P, E % P

    def runs():
        for b in range(B):
            n = min(P, full - b * P)
            if n > 0:
                yield slice(0, n), b, slice(0, P), b * P * P, n, P
        if rest:
            yield slice(full % P, full % P + 1), full // P, slice(0, rest), full * P, 1, rest

    with nc.Block() as block:
        @block.gpsimd
        def _(pool):
            for t in raw_i:
                nc.gpsimd.iota(t[:], pattern=[[P * P, B], [1, P]], base=0, channel_multiplier=P).then_inc(preset, 1)

        @block.sync
        def _(sp):
            sp.wait_ge(preset, 4)
            for rows, b, cols, at, n, w in runs():
                for field, t in ((a["src"], raw_i[0]), (a["dst"], raw_i[1]), (a["edge_weight"], raw[2])):
                    sp.dma_start(t[rows, b, cols], field[at:at + n * w].rearrange("(n w) -> n w", w=w)).then_inc(landed, 16)
                sp.dma_start(pair[rows, b, cols, :].rearrange("n w c -> n (w c)"),
                             a["edge_attr_2"][at:at + n * w, :].rearrange("(n w) c -> n (w c)", w=w)).then_inc(landed, 16)

        @block.vector
        def _(dve):
            nc.vector.memset(raw[2][:], 0.0).then_inc(preset, 1)
            nc.vector.memset(pair[:], 0.0).then_inc(preset, 1)
            dve.wait_ge(landed, 64 * len(list(runs())))
            for n in range(2):
                nc.vector.tensor_copy(raw[n][:], raw_i[n][:]).then_inc(cast, 1)
            for n in range(2):
                nc.vector.tensor_copy(part[n][:], pair[:, :, :, n]).then_inc(cast, 1)
            for n in range(5):
                dve.wait_ge(turn, n + 1)
                nc.vector.tensor_copy(k.fields[:, :, n], turned[n][:]).then_inc(s_done, 1)

        @block.tensor
        def _(pe):
            pe.wait_ge(cast, 4)
            pe.wait_ge(landed, 64 * len(list(runs())))
            for n, t in enumerate([raw[0], raw[1], raw[2], part[0], part[1]]):
                for b in range(B):
                    ins = nc.tensor.transpose(turned[n][:, b * P:(b + 1) * P], t[:, b, :], k.ident[:])
                ins.then_inc(turn, 1)
    ph.close()


def rank_phase(nc, k, name, key, payload, width, target, pos_out=None):
    ph = Phase(nc, name)
    NI, NT, NTH = k.NT // U, k.NT, k.NT
    key_i, part_i = ph.sb("key_i", [P, k.TC], I32), ph.sb("part_i", [P, k.TC], I32)
    high, low = ph.sb("high", [P, k.TC]), ph.sb("low", [P, k.TC])
    at_high = [ph.sb(f"at_high{n}", [P, NTH], BF16) for n in range(U)]
    at_low = [ph.sb(f"at_low{n}", [P, P], BF16) for n in range(U)]
    low_t = [ph.sb(f"low_t{n}", [P, P]) for n in range(2)]
    low_tb = [ph.sb(f"low_tb{n}", [P, P], BF16) for n in range(2)]
    earlier = [ph.sb(f"earlier{n}", [P, P], BF16) for n in range(2)]
    starts = [ph.sb(f"starts{n}", [P, NTH]) for n in range(2)]
    counts, below, upto, zeros = (ph.sb(n, [P, NTH]) for n in ("counts", "below", "upto", "zeros"))
    picked = [ph.sb(f"picked{n}", [P, NTH], BF16) for n in range(2)]
    rank_f, rank_i = ph.sb("rank_f", [P, U]), ph.sb("rank_i", [P, U], I32)
    row = ph.sb("row", [P, U, width])
    p_turn = [ph.ps(f"turn{n}", [P, 1024], BF16) for n in range(2)]
    p_same = [ph.ps(f"same{n}", [P, 512]) for n in range(2)]
    p_count = p_same[0][:, 0:NTH]
    p_rank = [ph.ps(f"rank{n}", [P, 512]) for n in range(2)]
    p_add = [ph.ps(f"add{n}", [P, 512]) for n in range(2)]
    digits, hist_hot, hist_mm = ph.sem("digits"), ph.sem("hist_hot"), ph.sem("hist_mm")
    prefix, prefix_mm, low_hot, high_hot = ph.sem("prefix"), ph.sem("prefix_mm"), ph.sem("low_hot"), ph.sem("high_hot")
    turned, copied, same, masked = ph.sem("turned"), ph.sem("copied"), ph.sem("same"), ph.sem("masked")
    ranked, added, advanced, picked_n = ph.sem("ranked"), ph.sem("added"), ph.sem("advanced"), ph.sem("picked_n")
    index_ready, row_ready, turn_pool = ph.sem("index_ready"), ph.sem("row_ready"), ph.sem("turn_pool")
    stored = ph.sem_per_slot("stored")
    rank_kept = ph.sem("rank_kept")

    def hots(i, j, first, which, sem_low, sem_high, mm):
        t = i * U + j
        nc.vector.tensor_scalar(at_low[j][:], k.ramp[:, 0:P], columns(low, t), None, ALU.is_equal).then_inc(sem_low, 1)
        nc.vector.tensor_scalar(at_high[j][:], k.ramp[:, 0:NTH], columns(high, t), None, ALU.is_equal).then_inc(sem_high, 1)

    with nc.Block() as block:
        @block.vector
        def _(dve):
            chain = Chain(dve, digits)
            chain(nc.vector.memset(zeros[:], 0.0))
            chain(nc.vector.tensor_copy(key_i[:], key))
            chain(nc.vector.tensor_scalar(part_i[:], key_i[:], 7, None, ALU.logical_shift_right))
            chain(nc.vector.tensor_copy(high[:], part_i[:]))
            chain(nc.vector.tensor_scalar(part_i[:], key_i[:], P - 1, None, ALU.bitwise_and))
            chain(nc.vector.tensor_copy(low[:], part_i[:]))

            def histogram(i, first):
                for j in range(U):
                    if not first:
                        dve.wait_ge(hist_mm, i * U + j - U + 1)
                    hots(i, j, first, 0, hist_hot, hist_hot, hist_mm)

            peeled(dve, NI, histogram)
            dve.wait_ge(hist_mm, NT)
            base = chain.n
            chain(nc.vector.tensor_copy(counts[:], p_count))
            dve.wait_ge(prefix_mm, 1)
            chain(nc.vector.tensor_copy(below[:], p_rank[0][:, 0:NTH]))
            chain(nc.vector.tensor_tensor_scan(upto[:], p_rank[1][:, 0:NTH], zeros[:], 0.0, ALU.add, ALU.add))
            chain(nc.vector.tensor_tensor(below[:], below[:], upto[:], ALU.add))
            chain(nc.vector.tensor_tensor(starts[0][:], below[:], p_rank[1][:, 0:NTH], ALU.subtract))
            dve.sem_inc(prefix, 1)

            def tiles(i, first):
                for j in range(U):
                    t = i * U + j
                    if not first:
                        dve.wait_ge(ranked, t - U + 1)
                        dve.wait_ge(added, t - U + 1)
                        dve.wait_ge(picked_n, t - U + 1)
                    hots(i, j, first, 0, low_hot, high_hot, None)
                for j in range(U):
                    t = i * U + j
                    dve.wait_ge(same, t + 1)
                    if not first or j >= 2:
                        dve.wait_ge(ranked, t - 1)
                    nc.vector.tensor_tensor(earlier[j % 2][:], p_same[j % 2][:, 0:P], k.before[:], ALU.mult).then_inc(masked, 1)
                    dve.wait_ge(added, t + 1)
                    if not first or j >= 1:
                        dve.wait_ge(ranked, t)
                        dve.wait_ge(advanced, t)
                    nc.vector.tensor_tensor(starts[(j + 1) % 2][:], starts[j % 2][:], p_add[j % 2][:, 0:NTH],
                                            ALU.add).then_inc(advanced, 1)
                    dve.wait_ge(ranked, t + 1)
                    dve.wait_ge(high_hot, t + 1)
                    if not first or j >= 2:
                        dve.wait_ge(picked_n, t - 1)
                    if not first:
                        dve.wait_ge(index_ready, t - U + 1)
                    nc.vector.tensor_tensor_reduce(picked[j % 2][:], at_high[j][:], p_rank[j % 2][:, 0:NTH], 1.0, 0.0,
                                                   ALU.mult, ALU.add, rank_f[:, j:j + 1]).then_inc(picked_n, 1)
                    dve.wait_ge(picked_n, t + 1)
                    if not first:
                        dve.wait_ge(stored[j], i * 16)
                    nc.vector.tensor_copy(rank_i[:, j:j + 1], rank_f[:, j:j + 1]).then_inc(index_ready, 1)
                if pos_out is not None:
                    dve.wait_ge(index_ready, i * U + U)
                    nc.vector.tensor_copy(columns(pos_out, i * U, U), rank_i[:]).then_inc(rank_kept, 1)

            peeled(dve, NI, tiles)

        @block.tensor
        def _(pe):
            def histogram(i, first):
                for j in range(U):
                    pe.wait_ge(hist_hot, (i * U + j + 1) * 2)
                    nc.tensor.matmul(p_count, at_low[j][:], at_high[j][:], start=first and j == 0, stop=False,
                                     skip_group_check=True).then_inc(hist_mm, 1)

            peeled(pe, NI, histogram)
            pe.wait_ge(digits, 7)
            nc.tensor.matmul(p_rank[0][:, 0:NTH], k.before[:], counts[:], start=True, stop=True)
            nc.tensor.matmul(p_rank[1][:, 0:NTH], k.ones[:], counts[:], start=True, stop=True).then_inc(prefix_mm, 1)

            def tiles(i, first):
                def head(j):
                    t = i * U + j
                    pe.wait_ge(low_hot, t + 1)
                    if not first or j >= 2:
                        pe.wait_ge(copied, 2 * (t - 1))
                    nc.tensor.transpose(p_turn[j % 2][:, 0:P], at_low[j][:], k.ident_bf[:]).then_inc(turned, 1)

                head(0)
                for j in range(U):
                    t = i * U + j
                    if j + 1 < U:
                        head(j + 1)
                    pe.wait_ge(copied, 2 * (t + 1))
                    if not first or j >= 2:
                        pe.wait_ge(masked, t - 1)
                    nc.tensor.matmul(p_same[j % 2][:, 0:P], low_tb[j % 2][:], low_tb[j % 2][:], start=True,
                                     stop=True).then_inc(same, 1)
                    pe.wait_ge(high_hot, t + 1)
                    if first and j == 0:
                        pe.wait_ge(prefix, 1)
                    if not first or j >= 2:
                        pe.wait_ge(advanced, t - 1)
                    nc.tensor.matmul(p_add[j % 2][:, 0:NTH], at_low[j][:], at_high[j][:], start=True,
                                     stop=True).then_inc(added, 1)
                    if not first or j >= 2:
                        pe.wait_ge(picked_n, t - 1)
                    if not first or j >= 1:
                        pe.wait_ge(advanced, t)
                    nc.tensor.matmul(p_rank[j % 2][:, 0:NTH], low_t[j % 2][:], starts[j % 2][:], start=True, stop=False)
                    pe.wait_ge(masked, t + 1)
                    nc.tensor.matmul(p_rank[j % 2][:, 0:NTH], earlier[j % 2][:], at_high[j][:], start=False,
                                     stop=True).then_inc(ranked, 1)

            peeled(pe, NI, tiles)

        @block.scalar
        def _(act):
            def tiles(i, first):
                for j in range(U):
                    t = i * U + j
                    act.wait_ge(turned, t + 1)
                    if not first or j >= 2:
                        act.wait_ge(ranked, t - 1)
                        act.wait_ge(same, t - 1)
                    nc.scalar.copy(low_tb[j % 2][:], p_turn[j % 2][:, 0:P]).then_inc(copied, 1)
                    nc.scalar.copy(low_t[j % 2][:], p_turn[j % 2][:, 0:P]).then_inc(copied, 1)
                    if not first:
                        act.wait_ge(stored[j], i * 16)
                    nc.scalar.copy(row[:, j, :], payload(t)).then_inc(row_ready, 1)

            peeled(act, NI, tiles)

        @block.gpsimd
        def _(pool):
            def tiles(i, first):
                for j in range(U):
                    t = i * U + j
                    pool.wait_ge(index_ready, t + 1)
                    pool.sem_inc(turn_pool, 1)
                    pool.wait_ge(row_ready, t + 1)
                    pool.sem_inc(turn_pool, 1)
                    nc.gpsimd.indirect_dma_start(target, bass.IndirectOffsetOnAxis(rank_i[:, j:j + 1], 0), row[:, j, :],
                                                 None, bounds_check=k.NP - 1, oob_is_err=False).then_inc(stored[j], 16)

            peeled(pool, NI, tiles)
            for j in range(U):
                pool.wait_ge(stored[j], NI * 16)
    ph.close()
def segments(nc, k, name, keys, rows, width, same_prev, same_next, whole):
    ph = Phase(nc, name)
    B = whole.shape[1]
    key = ph.sb("key", [P, B, width])
    prev, nxt = ph.sb("prev", [P, B]), ph.sb("next", [P, B])
    preset, landed, s_done = ph.sem("preset"), ph.sem("landed"), ph.sem("done")
    table = keys.rearrange("(r w) -> r w", w=width)
    n_dma = 0
    for b in range(B):
        n = min(P, rows - b * P)
        n_dma += 1 + (n - (b == 0) > 0) + (min(n, rows - b * P - 1) > 0)
    with nc.Block() as block:
        @block.sync
        def _(sp):
            sp.wait_ge(preset, 3)
            for b in range(B):
                r, n = b * P, min(P, rows - b * P)
                sp.dma_start(key[0:n, b, :], table[r:r + n, :]).then_inc(landed, 16)
                a = 1 if b == 0 else 0
                if n > a:
                    sp.dma_start(prev[a:n, b:b + 1], table[r + a - 1:r + n - 1, width - 1:width],
                                 allow_slow_non_contiguous=True).then_inc(landed, 16)
                m = min(n, rows - r - 1)
                if m > 0:
                    sp.dma_start(nxt[0:m, b:b + 1], table[r + 1:r + 1 + m, 0:1],
                                 allow_slow_non_contiguous=True).then_inc(landed, 16)

        @block.vector
        def _(dve):
            nc.vector.memset(key[:], -5.0).then_inc(preset, 1)
            nc.vector.memset(prev[:], -1.0).then_inc(preset, 1)
            nc.vector.memset(nxt[:], -2.0).then_inc(preset, 1)
            dve.wait_ge(landed, 16 * n_dma)
            last = width - 1
            for out, a0, a1 in ((same_prev[:, :, 1:width], key[:, :, 1:width], key[:, :, 0:last]),
                                (same_prev[:, :, 0], key[:, :, 0], prev[:]),
                                (same_next[:, :, 0:last], key[:, :, 0:last], key[:, :, 1:width]),
                                (same_next[:, :, last], key[:, :, last], nxt[:]),
                                (whole[:], key[:, :, 0], key[:, :, last])):
                nc.vector.tensor_tensor(out, a0, a1, ALU.is_equal).then_inc(s_done, 1)
    ph.close()


def segment_reduce(nc, k, name, val, same_prev, same_next, whole, op, out):
    ph = Phase(nc, name)
    B, W = whole.shape[1], val.shape[2]
    most = op == "max"
    none = -FAR if most else 0.0
    step, join = (ALU.add, ALU.max) if most else (ALU.mult, ALU.add)
    go_f, go_b, go_w = ph.sb("go_f", [P, B, W]), ph.sb("go_b", [P, B, W]), ph.sb("go_w", [P, B])
    fwd, bwd = ph.sb("fwd", [P, B, W]), ph.sb("bwd", [P, B, W])
    ends = ph.sb("ends", [P, 6, B])
    rows = ph.sb("rows", [1, 6, B * P])
    total = ph.sb("total", [1, 2, B * P])
    carry_row = ph.sb("carry_row", [1, 2, B * P])
    carry = ph.sb("carry", [P, 2, B])
    p_rows = [ph.ps(f"rows{n}", [P, 512]) for n in range(6)]
    p_carry = ph.ps("p_carry", [P, 512])
    step_done, ends_out, rows_in = ph.sem("step"), ph.sem("ends_out"), ph.sem("rows_in")
    F, L = slice(0, W), W - 1

    def scans(chain, init_f, init_b):
        for b in range(B):
            nc.vector.tensor_tensor_scan(fwd[:, b, :], go_f[:, b, :], val[:, b, :], init_f(b), step, join)
            ins = nc.vector.tensor_tensor_scan(bwd[:, b, ::-1], go_b[:, b, ::-1], val[:, b, ::-1], init_b(b), step, join)
            chain(ins)

    with nc.Block() as block:
        @block.vector
        def _(dve):
            chain = Chain(dve, step_done)
            for t, s in ((go_f, same_prev), (go_b, same_next), (go_w, whole)):
                if most:
                    chain(nc.vector.tensor_scalar(t[:], s[:], -1.0, FAR, ALU.add, ALU.mult))
                else:
                    chain(nc.vector.tensor_copy(t[:], s[:]))
            scans(chain, lambda b: none, lambda b: none)
            chain(nc.vector.tensor_copy(ends[:, 0, :], fwd[:, :, L]))
            chain(nc.vector.tensor_copy(ends[:, 3, :], bwd[:, :, 0]))
            chain(nc.vector.tensor_tensor(ends[:, 1, :], go_f[:, :, 0], go_w[:], step))
            chain(nc.vector.tensor_tensor(ends[:, 4, :], go_b[:, :, L], go_w[:], step))
            chain(nc.vector.tensor_copy(ends[:, 2, :], go_f[:, :, 0]))
            chain(nc.vector.tensor_copy(ends[:, 5, :], go_b[:, :, L]))
            dve.sem_inc(ends_out, 1)
            dve.wait_ge(rows_in, 1)
            for n in range(6):
                chain(nc.vector.tensor_copy(rows[:, n, :], p_rows[n][0:1, 0:B * P]))
            chain(nc.vector.tensor_tensor_scan(total[:, 0, :], rows[:, 1, :], rows[:, 0, :], none, step, join))
            chain(nc.vector.tensor_tensor_scan(total[:, 1, ::-1], rows[:, 4, ::-1], rows[:, 3, ::-1], none, step, join))
            chain(nc.vector.memset(carry_row[:], none))
            n = B * P
            chain(nc.vector.tensor_tensor(carry_row[:, 0, 1:n], rows[:, 2, 1:n], total[:, 0, 0:n - 1], step))
            chain(nc.vector.tensor_tensor(carry_row[:, 1, 0:n - 1], rows[:, 5, 0:n - 1], total[:, 1, 1:n], step))
            dve.sem_inc(ends_out, 1)
            dve.wait_ge(rows_in, 2)
            chain(nc.vector.tensor_copy(carry[:].rearrange("p s b -> p (s b)"), p_carry[:, 0:2 * B]))
            scans(chain, lambda b: carry[:, 0, b:b + 1], lambda b: carry[:, 1, b:b + 1])
            if most:
                chain(nc.vector.tensor_tensor(out[:], fwd[:], bwd[:], ALU.max))
            else:
                chain(nc.vector.tensor_tensor(out[:], fwd[:], bwd[:], ALU.add))
                chain(nc.vector.tensor_tensor(out[:], out[:], val[:], ALU.subtract))

        @block.tensor
        def _(pe):
            pe.wait_ge(ends_out, 1)
            for n in range(6):
                for b in range(B):
                    ins = nc.tensor.transpose(p_rows[n][0:1, b * P:(b + 1) * P], ends[:, n, b:b + 1], k.ident[:])
            ins.then_inc(rows_in, 1)
            pe.wait_ge(ends_out, 2)
            for s in range(2):
                for b in range(B):
                    ins = nc.tensor.transpose(p_carry[:, s * B + b:s * B + b + 1], carry_row[0:1, s, b * P:(b + 1) * P],
                                              k.ident[0:1, 0:1])
            ins.then_inc(rows_in, 1)
    ph.close()


def sorted_edges(nc, k, sorted_rows, dst_keys):
    ph = Phase(nc, "sorted")
    B, NT = k.TC // P, k.NT
    got = ph.sb("got", [P, B, P, 5])
    field = [ph.sb(f"field{n}", [P, B, P]) for n in range(5)]
    turned = [ph.ps(f"turned{n}", [P, B * P]) for n in range(5)]
    preset, landed, split, turn, s_done, kept = (ph.sem(n) for n in ("preset", "landed", "split", "turn", "done", "kept"))
    with nc.Block() as block:
        @block.sync
        def _(sp):
            sp.wait_ge(preset, 1)
            for b in range(B):
                n = min(P, NT - b * P)
                sp.dma_start(got[0:n, b, :, :].rearrange("a p f -> a (p f)"),
                             sorted_rows[b * P * P:(b * P + n) * P, :].rearrange("(a p) f -> a (p f)", p=P)).then_inc(landed, 16)
            sp.wait_ge(split, 5)
            for b in range(B):
                n = min(P, NT - b * P)
                sp.dma_start(dst_keys[b * P * P:(b * P + n) * P].rearrange("(a p) -> a p", p=P),
                             field[1][0:n, b, :]).then_inc(kept, 16)
            sp.wait_ge(kept, 16 * B)

        @block.vector
        def _(dve):
            nc.vector.memset(got[:], 0.0).then_inc(preset, 1)
            dve.wait_ge(landed, 16 * B)
            for n in range(5):
                nc.vector.tensor_copy(field[n][:], got[:, :, :, n]).then_inc(split, 1)
            for n in range(5):
                dve.wait_ge(turn, n + 1)
                nc.vector.tensor_copy(k.fields[:, :, n], turned[n][:]).then_inc(s_done, 1)

        @block.tensor
        def _(pe):
            for n in range(5):
                pe.wait_ge(split, n + 1)
                for b in range(B):
                    ins = nc.tensor.transpose(turned[n][:, b * P:(b + 1) * P], field[n][:, b, :], k.ident[:])
                ins.then_inc(turn, 1)
    ph.close()


def edge_columns(nc, k):
    ph = Phase(nc, "columns")
    B, TC = k.TC // P, k.TC
    last_t = ph.sb("last_t", [P, B, P])
    is_last, at, tmp = ph.sb("is_last", [P, TC]), ph.sb("at", [P, TC]), ph.sb("tmp", [P, TC])
    bottom = ph.sb("bottom", [P, 1])
    p_turn = ph.ps("p_turn", [P, TC])
    step, turn, turned = ph.sem("step"), ph.sem("turn"), ph.sem("turned")
    with nc.Block() as block:
        @block.vector
        def _(dve):
            chain = Chain(dve, step)
            chain(nc.vector.tensor_copy(k.src_i[:], k.fields[:, :, 0]))
            chain(nc.vector.tensor_copy(k.dst_i[:], k.fields[:, :, 1]))
            chain(nc.vector.tensor_scalar(last_t[:], k.d_next[:], -1.0, 1.0, ALU.mult, ALU.add))
            dve.sem_inc(turn, 1)
            dve.wait_ge(turned, 1)
            chain(nc.vector.tensor_copy(is_last[:], p_turn[:]))
            chain(nc.vector.tensor_scalar(at[:], k.fields[:, :, 1], float(-SKIP), None, ALU.add))
            chain(nc.vector.tensor_tensor(at[:], at[:], is_last[:], ALU.mult))
            chain(nc.vector.tensor_scalar(at[:], at[:], float(SKIP), None, ALU.add))
            chain(nc.vector.tensor_copy(k.put_i[:], at[:]))
            chain(nc.vector.memset(k.dst_before[:], -1.0))
            chain(nc.vector.tensor_copy(bottom[:], k.ident[:, P - 1:P]))
            chain(nc.vector.tensor_scalar(tmp[:], k.fields[:, :, 1], 1.0, None, ALU.add))
            chain(nc.vector.tensor_scalar(k.dst_before[:, 1:TC], tmp[:, 0:TC - 1], bottom[:], -1.0, ALU.mult, ALU.add))

        @block.tensor
        def _(pe):
            pe.wait_ge(turn, 1)
            for b in range(B):
                ins = nc.tensor.transpose(p_turn[:, b * P:(b + 1) * P], last_t[:, b, :], k.ident[:])
            ins.then_inc(turned, 1)
    ph.close()


def clear_table(nc, k, table):
    ph = Phase(nc, "clear")
    n = 8
    zeros = ph.sb("zeros", [P, n * AGG_W])
    ready, cleared = ph.sem("ready"), ph.sem("cleared")
    with nc.Block() as block:
        @block.gpsimd
        def _(pool):
            nc.gpsimd.memset(zeros[:], 0.0).then_inc(ready, 1)

        @block.sync
        def _(sp):
            sp.wait_ge(ready, 1)
            with sp.Fori(0, k.NP // (P * n)) as i:
                sp.dma_start(table[bass.ds(i * (P * n), P * n), :].rearrange("(p n) f -> p (n f)", n=n),
                             zeros[:]).then_inc(cleared, 16)
            sp.wait_ge(cleared, 16 * (k.NP // (P * n)))
    ph.close()


def aggregate(nc, k, name, agg, table=None, weight=None, ones=False, alpha=None, heads=None):
    ph = Phase(nc, name)
    NI, LAG = k.NT // U, 4
    assert NI > 1
    width = AGG_W
    cols = AGG_W if heads else (D + 1 if ones else D)
    dst_row = ph.sb("dst_row", [P, U, P])
    rows = ph.sb("rows", [P, U, cols])
    mix = [ph.sb(f"mix{j}", [P, P]) for j in range(U)]
    hand_on = [ph.sb(f"hand_on{j}", [P, P]) for j in range(U)]
    total = ph.sb("total", [P, U, width])
    take_i, put_i, pos_i = (ph.sb(n, [P, U], I32) for n in ("take_i", "put_i", "pos_i"))
    share = ph.sb("share", [P, U])
    p_sum = [ph.ps(f"sum{n}", [P, 512]) for n in range(4)]
    preset, mixed, summed, kept = ph.sem("preset"), ph.sem("mixed"), ph.sem("summed"), ph.sem("kept")
    indexed, turn_pool = ph.sem("indexed"), ph.sem("turn_pool")
    row_in, taken, put = ph.sem_per_slot("row_in"), ph.sem_per_slot("taken"), ph.sem_per_slot("put")
    share_in = ph.sem_per_slot("share_in") if alpha is not None else None
    keys = k.dst_keys
    n_preset = 1 + bool(ones)

    with nc.Block() as block:
        @block.sync
        def _(sp):
            def tiles(i, first):
                for j in range(U):
                    t = i * U + j
                    if not first:
                        sp.wait_ge(mixed, t - U + 1)
                    sp.dma_start(dst_row[:, j, :], keys[bass.ds(t * P, P)].rearrange("(a q) -> a q", a=1)
                                 .to_broadcast([P, P])).then_inc(row_in[j], 16)
            peeled(sp, NI, tiles)

        @block.vector
        def _(dve):
            nc.vector.memset(total[:], 0.0).then_inc(preset, 1)
            if ones:
                nc.vector.memset(rows[:, :, D:D + 1], 1.0).then_inc(preset, 1)

            def tiles(i, first):
                for j in range(U):
                    t = i * U + j
                    dve.wait_ge(row_in[j], 16 * (i + 1))
                    if not first:
                        dve.wait_ge(summed, t - U + 1)
                    if alpha is not None:
                        dve.wait_ge(share_in[j], 16 * (i + 1))
                    if heads:
                        nc.vector.tensor_scalar(mix[j][:], dst_row[:, j, :], k.dst_f(t), None, ALU.is_equal)
                        message, power = heads
                        nc.vector.tensor_tensor(
                            rows[:, j, :].rearrange("p (h f) -> p h f", h=4),
                            message(t).rearrange("p (o f) -> p o f", o=1).to_broadcast([P, 4, 65]),
                            power(t).rearrange("p (h o) -> p h o", o=1).to_broadcast([P, 4, 65]), ALU.mult)
                    else:
                        w = share[:, j:j + 1] if alpha is not None else weight(t)
                        nc.vector.tensor_scalar(mix[j][:], dst_row[:, j, :], k.dst_f(t), w, ALU.is_equal, ALU.mult)
                    nc.vector.tensor_scalar(hand_on[j][:], dst_row[:, j, :], columns(k.dst_before, t), None,
                                            ALU.is_equal).then_inc(mixed, 1)
            peeled(dve, NI, tiles)

        @block.tensor
        def _(pe):
            def tiles(i, first):
                for j in range(U):
                    t = i * U + j
                    pe.wait_ge(mixed, t + 1)
                    if table is not None:
                        pe.wait_ge(taken[j], 16 * (i + 1))
                    if first and j == 0:
                        pe.wait_ge(preset, n_preset)
                    if not first or j >= 4:
                        pe.wait_ge(kept, t - 3)
                    alone = first and j == 0
                    ins = nc.tensor.matmul(p_sum[j % 4][:, 0:cols], mix[j][:], rows[:, j, :], start=True, stop=alone)
                    if not alone:
                        pe.wait_ge(kept, t)
                        ins = nc.tensor.matmul(p_sum[j % 4][:, 0:cols], hand_on[j][:], total[:, (j - 1) % U, 0:cols],
                                               start=False, stop=True)
                    ins.then_inc(summed, 1)
            peeled(pe, NI, tiles)

        @block.scalar
        def _(act):
            def index(t, j, late):
                if late is not None and table is not None:
                    act.wait_ge(taken[j], 16 * late)
                if late is not None and alpha is not None:
                    act.wait_ge(share_in[j], 16 * late)
                if alpha is not None:
                    nc.scalar.copy(pos_i[:, j:j + 1], columns(k.pos_i, t))
                nc.scalar.copy(take_i[:, j:j + 1], columns(k.src_i, t)).then_inc(indexed, 1)

            for j in range(LAG):
                index(j, j, None)
            act.wait_ge(preset, n_preset)

            def tiles(i, first):
                for j in range(U):
                    t = i * U + j
                    act.wait_ge(summed, t + 1)
                    if not first:
                        act.wait_ge(put[j], 16 * i)
                    nc.scalar.copy(put_i[:, j:j + 1], columns(k.put_i, t))
                    nc.scalar.copy(total[:, j, 0:cols], p_sum[j % 4][:, 0:cols]).then_inc(kept, 1)
                    if j < U - LAG:
                        index(t + LAG, j + LAG, None if first else i)
                    else:
                        index(t + LAG, j + LAG - U, i + 1)
            peeled(act, NI, tiles)

        @block.gpsimd
        def _(pool):
            def store(t, j):
                pool.wait_ge(kept, t + 1)
                pool.sem_inc(turn_pool, 1)
                nc.gpsimd.indirect_dma_start(agg, bass.IndirectOffsetOnAxis(put_i[:, j:j + 1], 0), total[:, j, :],
                                             None, bounds_check=k.NP - 1, oob_is_err=False).then_inc(put[j], 16)

            def tiles(i, first):
                for j in range(U):
                    t = i * U + j
                    pool.wait_ge(indexed, t + 1)
                    pool.sem_inc(turn_pool, 1)
                    if alpha is not None:
                        if not first:
                            pool.wait_ge(mixed, t - U + 1)
                            pool.sem_inc(turn_pool, 1)
                        nc.gpsimd.indirect_dma_start(share[:, j:j + 1], None, alpha,
                                                     bass.IndirectOffsetOnAxis(pos_i[:, j:j + 1], 0)).then_inc(share_in[j], 16)
                    if table is not None:
                        if not first:
                            pool.wait_ge(summed, t - U + 1)
                            pool.sem_inc(turn_pool, 1)
                        nc.gpsimd.indirect_dma_start(rows[:, j, 0:D], None, table,
                                                     bass.IndirectOffsetOnAxis(take_i[:, j:j + 1], 0)).then_inc(taken[j], 16)
                    if not first or j >= LAG:
                        store(t - LAG, (j - LAG) % U)
            peeled(pool, NI, tiles)
            for j in range(U - LAG, U):
                store((NI - 1) * U + j, j)
            for j in range(U):
                pool.wait_ge(put[j], 16 * NI)
    ph.close()
G = 4
ROWS = G * P


class Steps(Chain):

    def __init__(self, engine, sem, turn, each):
        self.engine, self.sem, self.base, self.n, self.each = engine, sem, turn * each, 0, each

    def __call__(self, instruction):
        self.n += 1
        assert self.n <= self.each
        instruction.then_inc(self.sem, 1)
        self.engine.wait_ge(self.sem, self.base + self.n)

    def end(self):
        assert self.n == self.each, (self.n, self.each)


def group_rows(table, base, n=ROWS):
    return table[bass.ds(base, n), :].rearrange("(p g) f -> p g f", g=G)


def node_pass(nc, k, layer, x_in, x_out=None, agg=None, table_in=None, tables=()):
    ph = Phase(nc, f"node{layer}")
    NI = k.NT // U
    first_l, last_l = layer == 0, layer == 4
    widths = {0: (259,), 1: (2 * D,), 2: (2 * D, D), 3: (136,), 4: ()}[layer]
    x = [ph.sb(f"x{h}", [P, G, D]) for h in range(2)]
    if not first_l:
        sums = [ph.sb(f"sums{h}", [P, G, AGG_W]) for h in range(2)]
        xc = [ph.sb(f"xc{h}", [P, G, D]) for h in range(2)]
    if layer == 1:
        own_h = [ph.sb(f"own_h{h}", [P, G, D]) for h in range(2)]
        mixed_h = [ph.sb(f"mixed_h{h}", [P, G, D]) for h in range(2)]
        small = [[ph.sb(f"small{h}_{n}", [P, G]) for n in range(12)] for h in range(2)]
        half = ph.sb("half", [P, G])
    if last_l:
        den = [ph.sb(f"den{h}", [P, G, 4]) for h in range(2)]
        inv = [ph.sb(f"inv{h}", [P, G, 4]) for h in range(2)]
        scaled = [ph.sb(f"scaled{h}", [P, G, D]) for h in range(2)]
    if not last_l:
        xn = [ph.sb(f"xn{h}", [P, G, D]) for h in range(2)]
        stats = [ph.sb(f"stats{h}", [P, G, 6]) for h in range(2)]
        moments = [ph.sb(f"moments{h}", [P, G, 2]) for h in range(2)]
        var, inv_std = ([ph.sb(f"{n}{h}", [P, G]) for h in range(2)] for n in ("var", "inv_std"))
        minus_half = ph.sb("minus_half", [P, G])
        h_t = [ph.sb(f"h_t{n}", [P, D]) for n in range(G)]
        out = [ph.sb(f"out{h}", [P, G, sum(widths)]) for h in range(2)]
        junk = [ph.sb(f"junk{n}", [P, D]) for n in range(2)]
        p_turn = [ph.ps(f"p_turn{n}", [P, 512]) for n in range(2)]
        p_out = [[ph.ps(f"p_out{w}_{n}", [P, 512]) for n in range(2)] for w in range(len(widths))]
    if layer in (1, 2):
        xo = [ph.sb(f"xo{h}", [P, G, D]) for h in range(2)]
    if layer == 0:
        size2, gate, size2m, inv_size, scale = ([ph.sb(f"{n}{h}", [P, G]) for h in range(2)]
                                                for n in ("size2", "gate", "size2m", "inv_size", "scale"))
        rows_h = [ph.sb(f"rows_h{h}", [P, G, D]) for h in range(2)]
        pair_h = [ph.sb(f"pair_h{h}", [P, G, 2]) for h in range(2)]
    preset, pre, post = ph.sem("preset"), ph.sem("pre"), ph.sem("post")
    x_got, x_put = ph.sem_per_slot("x_got", 2), ph.sem_per_slot("x_put", 2)
    sums_got, own_got, t_put = (ph.sem_per_slot(n, 2) for n in ("sums_got", "own_got", "t_put"))
    joined, x_made = ph.sem("joined"), ph.sem("x_made")
    hc_made, squared, rooted, clamped, tanhed = (ph.sem(n) for n in ("hc_made", "squared", "rooted", "clamped", "tanhed"))
    var_made, std_made, normed, turned, rectified = (ph.sem(n) for n in ("var_made", "std_made", "normed", "turned", "rectified"))
    product, out_made, gated, sized, powered = (ph.sem(n) for n in ("product", "out_made", "gated", "sized", "powered"))
    scaled_by, stats_in = ph.sem("scaled_by"), ph.sem("stats_in")

    def x_ready(H):
        return {1: (x_made, H + 1), 2: (x_made, H + 1), 3: (joined, G * (H + 1)), 4: (joined, H + 1)}[layer]

    def halves(i, first, body):
        for h in range(2):
            body(i, h, i * 2 + h, first)

    def source(h):
        return x[h] if first_l else xc[h]

    with nc.Block() as block:
        @block.sync
        def _(sp):
            def load(i, h, H, first, last=False):
                if not first:
                    if last_l:
                        sp.wait_ge(joined, (H - 1))
                    elif first_l:
                        sp.wait_ge(normed, G * (H - 1))
                    else:
                        sp.wait_ge(joined, G * (H - 1))
                base = H * ROWS
                rows = ROWS
                if x_in.shape[0] == k.N:
                    if last:
                        rows = min(ROWS, k.N - base)
                        if rows <= 0:
                            base, rows = 0, ROWS
                sp.dma_start(x[h][0:rows // G], group_rows(x_in, base, rows)).then_inc(x_got[h], 16)
                if agg is not None:
                    sp.dma_start(sums[h][:], group_rows(agg, H * ROWS)).then_inc(sums_got[h], 16)
                if table_in is not None:
                    sp.dma_start(own_h[h][:], group_rows(table_in, H * ROWS)).then_inc(own_got[h], 16)

            def store(i, h, H, first, last=False):
                base = H * ROWS
                if x_out is not None:
                    rows = ROWS
                    if last and x_out.shape[0] == k.N:
                        rows = max(0, min(ROWS, k.N - base))
                    made = (xo if layer in (1, 2) else xc)[h]
                    sp.wait_ge(*x_ready(H))
                    if rows:
                        sp.dma_start(group_rows(x_out, base, rows), made[0:rows // G]).then_inc(x_put[h], 16)
                if layer == 0:
                    sp.wait_ge(out_made, H + 1)
                    sp.dma_start(group_rows(tables[0], base), rows_h[h][:]).then_inc(t_put[h], 16)
                    sp.dma_start(group_rows(tables[1], base), pair_h[h][:]).then_inc(t_put[h], 16)
                elif layer == 1:
                    sp.wait_ge(out_made, G * (H + 1))
                    sp.dma_start(group_rows(tables[0], base), out[h][:, :, 0:D]).then_inc(t_put[h], 16)
                elif layer == 2:
                    sp.wait_ge(out_made, G * (H + 1))
                    for n in range(3):
                        sp.dma_start(group_rows(tables[n], base), out[h][:, :, n * D:(n + 1) * D]).then_inc(t_put[h], 16)
                elif layer == 3:
                    sp.wait_ge(out_made, G * (H + 1))
                    sp.dma_start(group_rows(tables[0], base), out[h][:]).then_inc(t_put[h], 16)

            def step(i, first, last=False):
                load(i, 0, i * 2, first, last)
                if not first:
                    store(i - 1, 1, i * 2 - 1, first)
                load(i, 1, i * 2 + 1, first, last)
                store(i, 0, i * 2, first, last)

            if not last_l:
                sp.wait_ge(preset, 3)
            else:
                sp.wait_ge(preset, 2)
            step(0, True)
            if NI > 2:
                with sp.Fori(1, NI - 1) as i:
                    step(i, False)
            step(NI - 1, False, last=True)
            store(NI - 1, 1, NI * 2 - 1, False, last=True)
            n_t = {0: 2, 1: 1, 2: 3, 3: 1, 4: 0}[layer]
            for h in range(2):
                if n_t:
                    sp.wait_ge(t_put[h], 16 * n_t * NI)
                if x_out is not None:
                    short = last_l and (2 * NI - 2 + h) * ROWS >= k.N
                    sp.wait_ge(x_put[h], 16 * (NI - short))

        @block.vector
        def _(dve):
            for h in range(2):
                nc.vector.memset(x[h][:], 0.0).then_inc(preset, 1)
            if not last_l:
                nc.vector.memset(minus_half[:], -0.5).then_inc(preset, 1)
            if layer == 1:
                nc.vector.memset(half[:], 0.5).then_inc(preset, 1)

            def join(i, h, H, first):
                if first_l:
                    dve.wait_ge(x_got[h], 16 * (i + 1))
                    return
                if not first:
                    if layer in (1, 2):
                        dve.wait_ge(*x_ready(H - 2))
                    else:
                        dve.wait_ge(x_put[h], 16 * i)
                dve.wait_ge(x_got[h], 16 * (i + 1))
                dve.wait_ge(sums_got[h], 16 * (i + 1))
                if layer in (2, 3):
                    for g in range(G):
                        nc.vector.tensor_tensor(xc[h][:, g, :], x[h][:, g, :], sums[h][:, g, 0:D], ALU.add).then_inc(joined, 1)
                    dve.wait_ge(joined, G * (H + 1))
                    return
                if layer == 4:
                    steps = Steps(dve, pre, H, 3)
                    if not first:
                        dve.wait_ge(joined, H - 1)
                    steps(nc.vector.tensor_scalar(den[h][:], sums[h][:].rearrange("p g (n f) -> p g n f", n=4)[:, :, :, 64],
                                                  1e-10, None, ALU.add))
                    steps(nc.vector.reciprocal(inv[h][:], den[h][:]))
                    for g in range(G):
                        ins = nc.vector.tensor_tensor(
                            scaled[h][:, g, :].rearrange("p (n f) -> p n f", n=4),
                            sums[h][:, g, :].rearrange("p (n f) -> p n f", n=4)[:, :, 0:64],
                            inv[h][:, g, :].rearrange("p (n o) -> p n o", o=1).to_broadcast([P, 4, 64]), ALU.mult)
                    steps(ins)
                    steps.end()
                    for g in range(G):
                        ins = nc.vector.tensor_tensor(xc[h][:, g, :], x[h][:, g, :], scaled[h][:, g, :], ALU.add)
                    ins.then_inc(joined, 1)
                    dve.wait_ge(joined, H + 1)
                    return
                dve.wait_ge(own_got[h], 16 * (i + 1))
                s = small[h]
                steps = Steps(dve, pre, H, 10)
                steps(nc.vector.tensor_scalar(s[0][:], sums[h][:, :, D], 1e-10, None, ALU.add))
                steps(nc.vector.reciprocal(s[1][:], s[0][:]))
                for g in range(G):
                    nc.vector.scalar_tensor_tensor(mixed_h[h][:, g, :], sums[h][:, g, 0:D], s[1][:, g:g + 1],
                                                   own_h[h][:, g, :], ALU.mult, ALU.add).then_inc(hc_made, 1)
                dve.wait_ge(rooted, H + 1)
                nc.vector.tensor_scalar(s[3][:], s[4][:], 1e-15, None, ALU.max).then_inc(clamped, 1)
                dve.wait_ge(clamped, H + 1)
                steps(nc.vector.reciprocal(s[5][:], s[3][:]))
                dve.wait_ge(tanhed, H + 1)
                steps(nc.vector.tensor_tensor(s[7][:], s[6][:], s[5][:], ALU.mult))
                steps(nc.vector.tensor_tensor(s[8][:], s[7][:], s[4][:], ALU.mult))
                steps(nc.vector.tensor_scalar(s[9][:], s[8][:], 1e-8, None, ALU.add))
                steps(nc.vector.reciprocal(s[10][:], s[9][:]))
                steps(nc.vector.tensor_scalar(s[9][:], s[10][:], 0.95, -1.0, ALU.mult, ALU.add))
                steps(nc.vector.scalar_tensor_tensor(s[10][:], s[8][:], 0.95, s[9][:], ALU.is_gt, ALU.mult))
                steps(nc.vector.scalar_tensor_tensor(s[11][:], s[10][:], 1.0, s[7][:], ALU.add, ALU.mult))
                steps.end()
                dve.wait_ge(hc_made, G * (H + 1))
                for g in range(G):
                    nc.vector.scalar_tensor_tensor(xc[h][:, g, :], mixed_h[h][:, g, :], s[11][:, g:g + 1],
                                                   x[h][:, g, :], ALU.mult, ALU.add).then_inc(joined, 1)
                dve.wait_ge(joined, G * (H + 1))

            def norm(i, h, H, first):
                steps = Steps(dve, post, H, 2)
                if not first:
                    dve.wait_ge(std_made, H - 1)
                for g in range(G):
                    ins = nc.vector.bn_stats(stats[h][:, g, :], source(h)[:, g, :])
                steps(ins)
                dve.sem_inc(stats_in, 1)
                for g in range(G):
                    ins = nc.vector.bn_aggr(moments[h][:, g, :], stats[h][:, g, :])
                steps(ins)
                steps.end()
                nc.vector.tensor_scalar(var[h][:], moments[h][:, :, 1], 1e-5, None, ALU.add).then_inc(var_made, 1)
                dve.wait_ge(std_made, H + 1)
                for g in range(G):
                    if not first:
                        dve.wait_ge(turned, G * (H - 2) + g + 1)
                    nc.vector.tensor_scalar(xn[h][:, g, :], source(h)[:, g, :], moments[h][:, g, 0:1],
                                            inv_std[h][:, g:g + 1], ALU.subtract, ALU.mult).then_inc(normed, 1)

            def finish(i, h, H, first):
                if layer == 0:
                    dve.wait_ge(squared, G * (H + 1))
                    nc.vector.tensor_scalar(size2m[h][:], size2[h][:], 1e-24, None, ALU.max).then_inc(sized, 1)
                    dve.wait_ge(powered, H + 1)
                    dve.wait_ge(gated, H + 1)
                    nc.vector.scalar_tensor_tensor(scale[h][:], gate[h][:], 1.5, inv_size[h][:], ALU.mult,
                                                   ALU.mult).then_inc(scaled_by, 1)
                    dve.wait_ge(scaled_by, H + 1)
                    if not first:
                        dve.wait_ge(t_put[h], 32 * i)
                    for g in range(G):
                        nc.vector.tensor_scalar(rows_h[h][:, g, :], out[h][:, g, 0:D], scale[h][:, g:g + 1], None, ALU.mult)
                    nc.vector.tensor_tensor(pair_h[h][:], out[h][:, :, 257:259],
                                            scale[h][:].rearrange("p (g o) -> p g o", o=1).to_broadcast([P, G, 2]),
                                            ALU.mult).then_inc(out_made, 1)

            def step(i, first):
                for h in range(2):
                    H = i * 2 + h
                    join(i, h, H, first)
                    if not last_l:
                        norm(i, h, H, first)
                    if layer == 0:
                        if h == 0 and not first:
                            finish(i - 1, 1, H - 1, False)
                        if h == 1:
                            finish(i, 0, H - 1, first)

            peeled(dve, NI, step)
            if layer == 0:
                finish(NI - 1, 1, 2 * NI - 1, False)

        @block.gpsimd
        def _(pool):
            def step(i, first):
                for h in range(2):
                    H = i * 2 + h
                    if layer == 1:
                        pool.wait_ge(squared, G * (H + 1))
                        nc.gpsimd.tensor_tensor(small[h][4][:], small[h][2][:], half[:], ALU.pow).then_inc(rooted, 1)
                    if not last_l:
                        pool.wait_ge(var_made, H + 1)
                        if not first:
                            pool.wait_ge(normed, G * (H - 1))
                        nc.gpsimd.tensor_tensor(inv_std[h][:], var[h][:], minus_half[:], ALU.pow).then_inc(std_made, 1)
                    if layer == 0:
                        if h == 1 or not first:
                            power(H - 1, 1 - h)
                    if layer == 1:
                        if h == 1:
                            own(i, 0, H - 1, first)
                        elif not first:
                            own(i - 1, 1, H - 1, False)
                    if layer == 2:
                        if not first:
                            pool.wait_ge(x_put[h], 16 * i)
                        pool.wait_ge(joined, G * (H + 1))
                        for g in range(G):
                            ins = nc.gpsimd.tensor_tensor(xo[h][:, g, :], xc[h][:, g, :], k.fc_bias[:], ALU.add)
                        ins.then_inc(x_made, 1)

            def own(i, h, H, first):
                if not first:
                    pool.wait_ge(x_put[h], 16 * i)
                pool.wait_ge(out_made, G * (H + 1))
                for g in range(G):
                    ins = nc.gpsimd.tensor_tensor(xo[h][:, g, :], xc[h][:, g, :], out[h][:, g, D:2 * D], ALU.add)
                ins.then_inc(x_made, 1)

            def power(H, h):
                pool.wait_ge(sized, H + 1)
                nc.gpsimd.tensor_tensor(inv_size[h][:], size2m[h][:], minus_half[:], ALU.pow).then_inc(powered, 1)

            if not last_l:
                pool.wait_ge(preset, 4 if layer == 1 else 3)
                peeled(pool, NI, step)
            if layer == 0:
                power(2 * NI - 1, 1)
            if layer == 1:
                own(NI - 1, 1, 2 * NI - 1, False)

        @block.tensor
        def _(pe):
            def step(i, first):
                for h in range(2):
                    H = i * 2 + h

                    def turn(g):
                        t = G * H + g
                        pe.wait_ge(normed, t + 1)
                        if not (first and h == 0 and g < 2):
                            pe.wait_ge(rectified, t - 1)
                        for c in range(2):
                            ins = nc.tensor.transpose(p_turn[g % 2][:, c * P:(c + 1) * P], xn[h][:, g, c * P:(c + 1) * P],
                                                      k.ident[:])
                        ins.then_inc(turned, 1)

                    turn(0)
                    for g in range(G):
                        t = G * H + g
                        if g + 1 < G:
                            turn(g + 1)
                        pe.wait_ge(rectified, t + 1)
                        if not (first and h == 0 and g < 2):
                            pe.wait_ge(squared if layer == 0 else out_made, t - 1)
                        for w, (n, weights, bias) in enumerate(k.products[layer]):
                            for c in range(2):
                                ins = nc.tensor.matmul(p_out[w][g % 2][:, 0:n], h_t[g][:, c * P:(c + 1) * P], weights[:, c, :],
                                                       start=c == 0, stop=c == 1 and bias is None)
                            if bias is not None:
                                ins = nc.tensor.matmul(p_out[w][g % 2][:, 0:n], k.ones[0:1, :], bias, start=False, stop=True)
                        ins.then_inc(product, 1)
            if not last_l:
                peeled(pe, NI, step)

        @block.scalar
        def _(act):
            def step(i, first):
                for h in range(2):
                    H = i * 2 + h
                    if layer == 1:
                        for g in range(G):
                            act.wait_ge(hc_made, G * H + g + 1)
                            if not (first and h == 0 and g < 2):
                                act.wait_ge(squared, G * H + g - 1)
                            nc.scalar.activation(junk[g % 2][:], mixed_h[h][:, g, :], ACT.Square,
                                                 accum_out=small[h][2][:, g:g + 1]).then_inc(squared, 1)
                        act.wait_ge(clamped, H + 1)
                        nc.scalar.activation(small[h][6][:], small[h][3][:], ACT.Tanh).then_inc(tanhed, 1)

                    def rectify(g):
                        t = G * H + g
                        act.wait_ge(turned, t + 1)
                        if not (first and h == 0):
                            act.wait_ge(product, t - G + 1)
                        nc.scalar.activation(h_t[g][:], p_turn[g % 2][:, 0:D], ACT.Relu).then_inc(rectified, 1)

                    rectify(0)
                    for g in range(G):
                        t = G * H + g
                        if g + 1 < G:
                            rectify(g + 1)
                        if not first and g == 0:
                            if layer == 0:
                                act.wait_ge(out_made, H - 1)
                            else:
                                act.wait_ge(t_put[h], 16 * len(tables) * i)
                            if layer == 1:
                                act.wait_ge(x_made, H - 1)
                        act.wait_ge(product, t + 1)
                        if layer == 0:
                            nc.scalar.copy(out[h][:, g, :], p_out[0][g % 2][:, 0:259])
                            if not (first and h == 0 and g < 2):
                                act.wait_ge(squared, t - 1)
                            nc.scalar.activation(junk[g % 2][:], p_out[0][g % 2][:, 0:D], ACT.Square,
                                                 accum_out=size2[h][:, g:g + 1]).then_inc(squared, 1)
                        elif layer == 2:
                            nc.scalar.copy(out[h][:, g, 0:2 * D], p_out[0][g % 2][:])
                            nc.scalar.copy(out[h][:, g, 2 * D:3 * D], p_out[1][g % 2][:, 0:D]).then_inc(out_made, 1)
                        else:
                            nc.scalar.copy(out[h][:, g, 0:widths[0]], p_out[0][g % 2][:, 0:widths[0]]).then_inc(out_made, 1)
                    if layer == 0:
                        act.wait_ge(squared, G * (H + 1))
                        nc.scalar.activation(gate[h][:], out[h][:, :, 256], ACT.Sigmoid).then_inc(gated, 1)
            if not last_l:
                peeled(act, NI, step)
    ph.close()
def score_pass(nc, k, name, layer, table_src, table_dst=None, out=None, put=None, messages=None):
    ph = Phase(nc, name)
    NI, LAG = k.NT // U, 4
    W = {0: 2, 2: D, 3: 136}[layer]
    a = [ph.sb(f"a{j}", [P, W]) for j in range(U)]
    b = [ph.sb(f"b{j}", [P, W]) for j in range(U)] if table_dst is not None else None
    take_a, take_b, pos_i = (ph.sb(n, [P, U], I32) for n in ("take_a", "take_b", "pos_i"))
    z = [ph.sb(f"z{n}", [P, D]) for n in range(4)]
    score = ph.sb("score", [P, U])
    indexed, turn_pool, scored, step = (ph.sem(n) for n in ("indexed", "turn_pool", "scored", "step"))
    got_a, got_b, put_s = (ph.sem_per_slot(n) for n in ("got_a", "got_b", "put"))
    each = {0: 0, 2: 2, 3: 3}[layer]

    with nc.Block() as block:
        @block.scalar
        def _(act):
            def index(t, j, late):
                if late is not None:
                    act.wait_ge(got_a[j], 16 * late)
                    if b is not None:
                        act.wait_ge(got_b[j], 16 * late)
                nc.scalar.copy(take_a[:, j:j + 1], columns(k.src_i, t)).then_inc(indexed, 1)
                if b is not None:
                    nc.scalar.copy(take_b[:, j:j + 1], columns(k.dst_i, t)).then_inc(indexed, 1)

            for j in range(LAG):
                index(j, j, None)

            def tiles(i, first):
                for j in range(U):
                    t = i * U + j
                    if j < U - LAG:
                        index(t + LAG, j + LAG, None if first else i)
                    else:
                        index(t + LAG, j + LAG - U, i + 1)
            peeled(act, NI, tiles)

        @block.gpsimd
        def _(pool):
            def store(t, j):
                pool.wait_ge(scored, t + 1)
                pool.sem_inc(turn_pool, 1)
                nc.gpsimd.indirect_dma_start(put, bass.IndirectOffsetOnAxis(pos_i[:, j:j + 1], 0), score[:, j:j + 1],
                                             None, bounds_check=k.NP - 1, oob_is_err=False).then_inc(put_s[j], 16)

            def tiles(i, first):
                for j in range(U):
                    t = i * U + j
                    pool.wait_ge(indexed, (t + 1) * (1 if b is None else 2))
                    pool.sem_inc(turn_pool, 1)
                    if not first:
                        pool.wait_ge(scored, t - U + 1)
                        pool.sem_inc(turn_pool, 1)
                    nc.gpsimd.indirect_dma_start(a[j][:], None, table_src,
                                                 bass.IndirectOffsetOnAxis(take_a[:, j:j + 1], 0)).then_inc(got_a[j], 16)
                    if b is not None:
                        nc.gpsimd.indirect_dma_start(b[j][:], None, table_dst,
                                                     bass.IndirectOffsetOnAxis(take_b[:, j:j + 1], 0)).then_inc(got_b[j], 16)
                    if put is not None and (not first or j >= LAG):
                        store(t - LAG, (j - LAG) % U)
            peeled(pool, NI, tiles)
            if put is not None:
                for j in range(U - LAG, U):
                    store((NI - 1) * U + j, j)
                for j in range(U):
                    pool.wait_ge(put_s[j], 16 * NI)

        @block.vector
        def _(dve):
            def tiles(i, first):
                for j in range(U):
                    t = i * U + j
                    dve.wait_ge(got_a[j], 16 * (i + 1))
                    if b is not None:
                        dve.wait_ge(got_b[j], 16 * (i + 1))
                    s = Steps(dve, step, t, each)
                    z0, z1 = z[2 * (j % 2)], z[2 * (j % 2) + 1]
                    if layer == 0:
                        nc.vector.tensor_tensor(columns(out, t), a[j][:, 0:1], b[j][:, 1:2], ALU.add).then_inc(scored, 1)
                    elif layer == 2:
                        s(nc.vector.tensor_tensor(z0[:], a[j][:], b[j][:], ALU.add))
                        s(nc.vector.scalar_tensor_tensor(z1[:], z0[:], 0.2, z0[:], ALU.mult, ALU.max))
                        if not first:
                            dve.wait_ge(put_s[j], 16 * i)
                        nc.vector.tensor_copy(pos_i[:, j:j + 1], columns(k.pos_i, t))
                        nc.vector.tensor_tensor_reduce(z0[:], z1[:], k.attn[:], 1.0, 0.0, ALU.mult, ALU.add,
                                                       score[:, j:j + 1]).then_inc(scored, 1)
                    else:
                        fwd, rev = k.fields[:, bass.ds(t, 1), 3], k.fields[:, bass.ds(t, 1), 4]
                        nc.vector.tensor_scalar(z0[:, 0:64], a[j][:, 64:128], rev, None, ALU.mult)
                        s(nc.vector.tensor_scalar(z0[:, 64:68], a[j][:, 132:136], rev, None, ALU.mult))
                        nc.vector.scalar_tensor_tensor(messages[:, bass.ds(t, 1), 0:64].rearrange("p o f -> p (o f)"),
                                                       a[j][:, 0:64], fwd, z0[:, 0:64], ALU.mult, ALU.add)
                        s(nc.vector.scalar_tensor_tensor(z1[:, 0:4], a[j][:, 128:132], fwd, z0[:, 64:68], ALU.mult, ALU.add))
                        s(nc.vector.scalar_tensor_tensor(out[:, bass.ds(t, 1), :].rearrange("p o f -> p (o f)"),
                                                         z1[:, 0:4], 0.2, z1[:, 0:4], ALU.mult, ALU.max))
                        dve.sem_inc(scored, 1)
                    s.end()
            peeled(dve, NI, tiles)
    ph.close()


def to_rows(nc, k, name, cols, rows):
    ph = Phase(nc, name)
    p = ph.ps("p", [P, k.TC])
    turned, s_done = ph.sem("turned"), ph.sem("done")
    with nc.Block() as block:
        @block.tensor
        def _(pe):
            for b in range(k.TC // P):
                ins = nc.tensor.transpose(p[:, b * P:(b + 1) * P], cols[:, b * P:(b + 1) * P], k.ident[:])
            ins.then_inc(turned, 1)

        @block.vector
        def _(dve):
            dve.wait_ge(turned, 1)
            nc.vector.tensor_copy(rows[:].rearrange("p b q -> p (b q)"), p[:]).then_inc(s_done, 1)
    ph.close()


def powers(nc, k, name, rows, most, cols):
    ph = Phase(nc, name)
    less, power = ph.sb("less", [P, k.TC // P, P]), ph.sb("power", [P, k.TC // P, P])
    p = ph.ps("p", [P, k.TC])
    lessened, raised, turned, s_done = (ph.sem(n) for n in ("lessened", "raised", "turned", "done"))
    with nc.Block() as block:
        @block.vector
        def _(dve):
            nc.vector.tensor_tensor(less[:], rows[:], most[:], ALU.subtract).then_inc(lessened, 1)
            dve.wait_ge(turned, 1)
            nc.vector.tensor_copy(cols[:], p[:]).then_inc(s_done, 1)

        @block.scalar
        def _(act):
            act.wait_ge(lessened, 1)
            nc.scalar.activation(power[:], less[:], ACT.Exp).then_inc(raised, 1)

        @block.tensor
        def _(pe):
            pe.wait_ge(raised, 1)
            for b in range(k.TC // P):
                ins = nc.tensor.transpose(p[:, b * P:(b + 1) * P], power[:, b, :], k.ident[:])
            ins.then_inc(turned, 1)
    ph.close()


def shares_by_source(nc, k, keys, scores, shares):
    hold = Phase(nc, "by_src")
    W = k.NT
    same_prev, same_next = hold.sb("same_prev", [P, 1, W]), hold.sb("same_next", [P, 1, W])
    whole = hold.sb("whole", [P, 1])
    score, most, power, total, share = (hold.sb(n, [P, 1, W]) for n in ("score", "most", "power", "total", "share"))
    inverse = hold.sb("inverse", [P, 1, W])
    segments(nc, k, "src_seg", keys, P, W, same_prev, same_next, whole)
    ph = Phase(nc, "src_in")
    landed = ph.sem("landed")
    with nc.Block() as block:
        @block.sync
        def _(sp):
            sp.dma_start(score[:, 0, :], scores.rearrange("(r w) o -> r (w o)", w=W)).then_inc(landed, 16)
            sp.wait_ge(landed, 16)
    ph.close()
    segment_reduce(nc, k, "src_max", score, same_prev, same_next, whole, "max", most)
    ph = Phase(nc, "src_exp")
    lessened, raised = ph.sem("lessened"), ph.sem("raised")
    with nc.Block() as block:
        @block.vector
        def _(dve):
            nc.vector.tensor_tensor(total[:], score[:], most[:], ALU.subtract).then_inc(lessened, 1)

        @block.scalar
        def _(act):
            act.wait_ge(lessened, 1)
            nc.scalar.activation(power[:], total[:], ACT.Exp).then_inc(raised, 1)
    ph.close()
    segment_reduce(nc, k, "src_sum", power, same_prev, same_next, whole, "sum", total)
    ph = Phase(nc, "src_out")
    step, stored = ph.sem("step"), ph.sem("stored")
    with nc.Block() as block:
        @block.vector
        def _(dve):
            chain = Chain(dve, step)
            chain(nc.vector.reciprocal(inverse[:], total[:]))
            chain(nc.vector.tensor_tensor(share[:], power[:], inverse[:], ALU.mult))

        @block.sync
        def _(sp):
            sp.wait_ge(step, 2)
            sp.dma_start(shares.rearrange("(r w) o -> r (w o)", w=W), share[:, 0, :]).then_inc(stored, 16)
            sp.wait_ge(stored, 16)
    ph.close()
    hold.close()


def head_powers(nc, k, scores, messages):
    ph = Phase(nc, "head_pow")
    NT = k.NT
    place_i, place = ph.sb("place_i", [P, NT], I32), ph.sb("place", [P, NT])
    far = ph.sb("far", [P, NT])
    most, all_most = ph.sb("most", [P, 4]), ph.sb("all_most", [P, 4])
    less = ph.sb("less", [P, NT, 4])
    counted, step, reduced, raised = (ph.sem(n) for n in ("counted", "step", "reduced", "raised"))
    with nc.Block() as block:
        @block.gpsimd
        def _(pool):
            nc.gpsimd.iota(place_i[:], pattern=[[P, NT]], base=0, channel_multiplier=1).then_inc(counted, 1)
            pool.wait_ge(step, 4)
            nc.gpsimd.partition_all_reduce(all_most[:], most[:], P, bass.bass_isa.ReduceOp.max).then_inc(reduced, 1)

        @block.vector
        def _(dve):
            chain = Chain(dve, step)
            dve.wait_ge(counted, 1)
            chain(nc.vector.tensor_copy(place[:], place_i[:]))
            chain(nc.vector.tensor_scalar(far[:], place[:], float(k.E), -FAR, ALU.is_ge, ALU.mult))
            chain(nc.vector.tensor_tensor(less[:], scores[:], far[:].rearrange("p (t o) -> p t o", o=1)
                                          .to_broadcast([P, NT, 4]), ALU.add))
            chain(nc.vector.tensor_reduce(most[:], less[:].rearrange("p t h -> p h t"), AX.X, ALU.max))
            dve.wait_ge(reduced, 1)
            chain(nc.vector.tensor_tensor(less[:], less[:], all_most[:].rearrange("p (o h) -> p o h", o=1)
                                          .to_broadcast([P, NT, 4]), ALU.subtract))
            chain(nc.vector.memset(messages[:, :, 64:65], 1.0))

        @block.scalar
        def _(act):
            act.wait_ge(step, 5)
            nc.scalar.activation(scores[:], less[:], ACT.Exp).then_inc(raised, 1)
    ph.close()


def weights(nc, k, a):
    ph = Phase(nc, "weights")
    square = [ph.sb(f"square{n}", [P, 2, D]) for n in range(4)]
    names = ["L0_gnn_W", "L2_gnn_W_s", "L2_gnn_W_t", "L2_gnn_W_fc"]
    flat = [ph.sb(f"flat{n}", [64, D]) for n in range(2)]
    attn0, bias0 = ph.sb("attn0", [P, 2, 2]), ph.sb("bias0", [P, 2])
    attn3 = ph.sb("attn3", [64, 4])
    p_turn = [ph.ps(f"p_turn{n}", [P, 512]) for n in range(4)]
    p_flat = ph.ps("p_flat", [P, 512])
    p_attn = ph.ps("p_attn", [P, 512])
    landed, turned, s_done = ph.sem("landed"), ph.sem("turned"), ph.sem("done")
    loads = [(square[n][:], a[name].rearrange("(d p) i -> p d i", p=P)) for n, name in enumerate(names)]
    loads += [(flat[0][:], a["L3_gnn_W_forward"]), (flat[1][:], a["L3_gnn_W_reverse"])]
    loads += [(k.w1[:, :, 0:D], a["L1_gnn_w_nbr"].rearrange("(c p) o -> p c o", p=P)),
              (k.w1[:, :, D:2 * D], a["L1_gnn_w_own"].rearrange("(c p) o -> p c o", p=P)),
              (k.b1[:, D:2 * D], a["L1_gnn_bias"].rearrange("(o f) -> o f", o=1)),
              (k.b0[:, 0:D], a["L0_gnn_b"].rearrange("(o f) -> o f", o=1)),
              (k.b0[:, D:D + 1], a["L0_gnn_mag_b"].rearrange("(o f) -> o f", o=1)),
              (k.attn[:], a["L2_gnn_W_attn"].to_broadcast([P, D])),
              (k.fc_bias[:], a["L2_gnn_b_fc"].rearrange("(o f) -> o f", o=1).to_broadcast([P, D]))]
    thin = [(k.w0[:, c, D:D + 1], a["L0_gnn_mag_w"][:, c * P:(c + 1) * P].rearrange("o p -> p o")) for c in range(2)]
    thin += [(attn0[:, d, s:s + 1], a["L0_gnn_attn_w"][:, s * D + d * P:s * D + (d + 1) * P].rearrange("o p -> p o"))
             for d in range(2) for s in range(2)]
    thin += [(bias0[:, d:d + 1], a["L0_gnn_b"][d * P:(d + 1) * P].rearrange("(p o) -> p o", o=1)) for d in range(2)]
    thin += [(attn3[:, n:n + 1], a["L3_gnn_attn_forward"][0, n:n + 1, :].rearrange("o p -> p o")) for n in range(4)]
    with nc.Block() as block:
        @block.sync
        def _(sp):
            for to, frm in loads + thin:
                sp.dma_start(to, frm, allow_slow_non_contiguous=True).then_inc(landed, 16)

        @block.tensor
        def _(pe):
            pe.wait_ge(landed, 16 * len(loads + thin))
            for n in range(4):
                for c in range(2):
                    for d in range(2):
                        nc.tensor.transpose(p_turn[n][:, c * D + d * P:c * D + (d + 1) * P],
                                            square[n][:, d, c * P:(c + 1) * P], k.ident[:])
            for n in range(2):
                for c in range(2):
                    nc.tensor.transpose(p_flat[:, (c * 2 + n) * 64:(c * 2 + n) * 64 + 64], flat[n][:, c * P:(c + 1) * P],
                                        k.ident[0:64, 0:64])
            for c in range(2):
                for d in range(2):
                    nc.tensor.matmul(p_attn[:, 2 * c:2 * c + 2], square[0][:, d, c * P:(c + 1) * P], attn0[:, d, :],
                                     start=d == 0, stop=d == 1)
                for n in range(2):
                    nc.tensor.matmul(p_attn[:, 8 + (c * 2 + n) * 4:12 + (c * 2 + n) * 4], flat[n][:, c * P:(c + 1) * P],
                                     attn3[:], start=True, stop=True)
            for d in range(2):
                ins = nc.tensor.matmul(p_attn[0:1, 4:6], bias0[:, d:d + 1], attn0[:, d, :], start=d == 0, stop=d == 1)
            ins.then_inc(turned, 1)

        @block.vector
        def _(dve):
            nc.vector.memset(k.b1[:, 0:D], 0.0).then_inc(s_done, 1)
            dve.wait_ge(turned, 1)
            to = [k.w0[:, :, 0:D], k.w2[:, :, 0:D], k.w2[:, :, D:2 * D], k.w2[:, :, 2 * D:3 * D]]
            for n in range(4):
                nc.vector.tensor_copy(to[n], p_turn[n][:].rearrange("p (c o) -> p c o", c=2)).then_inc(s_done, 1)
            nc.vector.tensor_copy(k.w3[:, :, 0:P], p_flat[:, 0:2 * P].rearrange("p (c o) -> p c o", c=2)).then_inc(s_done, 1)
            nc.vector.tensor_copy(k.w0[:, :, D + 1:D + 3], p_attn[:, 0:4].rearrange("p (c o) -> p c o", c=2)).then_inc(s_done, 1)
            nc.vector.tensor_copy(k.w3[:, :, P:P + 8], p_attn[:, 8:24].rearrange("p (c o) -> p c o", c=2)).then_inc(s_done, 1)
            nc.vector.tensor_copy(k.b0[:, D + 1:D + 3], p_attn[0:1, 4:6]).then_inc(s_done, 1)
    ph.close()


class Kept:
    pass


def gnn_kernel(nc, a, out, check=None):
    k = Kept()
    k.N, k.E = a["x"].shape[0], a["src"].shape[0]
    k.NT = -(-max(k.N, k.E) // (P * U)) * U
    k.NP = k.NT * P
    k.TC = -(-k.NT // P) * P
    B = k.TC // P
    assert k.N == k.E and k.N % G == 0

    def dram(name, shape):
        return nc.dram_tensor(name, shape, F32).ap()

    with ExitStack() as ctx:
        def sb(name, shape, dt=F32):
            return ctx.enter_context(nc.sbuf_tensor(name, shape, dt))

        k.ones, k.ident, k.before = sb("ones", [P, P]), sb("ident", [P, P]), sb("before", [P, P])
        k.ident_bf = sb("ident_bf", [P, P], BF16)
        k.ramp_i, k.ramp = sb("ramp_i", [P, k.TC], I32), sb("ramp", [P, k.TC])
        k.fields = sb("fields", [P, k.TC, 5])
        k.src_i, k.dst_i, k.put_i, k.pos_i = (sb(n, [P, k.TC], I32) for n in ("src_i", "dst_i", "put_i", "pos_i"))
        k.dst_before = sb("dst_before", [P, k.TC])
        k.d_prev, k.d_next, k.d_whole = sb("d_prev", [P, B, P]), sb("d_next", [P, B, P]), sb("d_whole", [P, B])
        k.w0, k.w1 = sb("w0", [P, 2, D + 3]), sb("w1", [P, 2, 2 * D])
        k.w2, k.w3 = sb("w2", [P, 2, 3 * D]), sb("w3", [P, 2, P + 8])
        k.b0, k.b1 = sb("b0", [1, D + 3]), sb("b1", [1, 2 * D])
        k.attn, k.fc_bias = sb("attn", [P, D]), sb("fc_bias", [P, D])
        k.dst_f = lambda t: k.fields[:, bass.ds(t, 1), 1]
        k.products = {0: [(D + 3, k.w0, k.b0[:])],
                      1: [(2 * D, k.w1, k.b1[:])],
                      2: [(2 * D, k.w2[:, :, 0:2 * D], None), (D, k.w2[:, :, 2 * D:3 * D], None)],
                      3: [(P + 8, k.w3, None)]}

        sorted_rows, k.dst_keys = dram("sorted_rows", (k.NP, 5)), dram("dst_keys", (k.NP,))
        src_keys, scores, shares = dram("src_keys", (k.NP, 1)), dram("scores", (k.NP, 1)), dram("shares", (k.NP, 1))
        agg = dram("agg", (k.NP, AGG_W))
        h0, ends0 = dram("h0", (k.NP, D)), dram("ends0", (k.NP, 2))
        h1, from_src, to_dst, h2, h3 = (dram(n, (k.NP, w)) for n, w in
                                        (("h1", D), ("from_src", D), ("to_dst", D), ("h2", D), ("h3", P + 8)))
        x1, x2, x3 = (dram(n, (k.NP, D)) for n in ("x1", "x2", "x3"))

        constants(nc, k)
        weights(nc, k, a)
        clear_table(nc, k, agg)
        load_edges(nc, k, a)
        rank_phase(nc, k, "by_dst", k.fields[:, :, 1],
                   lambda t: k.fields[:, bass.ds(t, 1), :].rearrange("p o f -> p (o f)"), 5, sorted_rows)
        sorted_edges(nc, k, sorted_rows, k.dst_keys)
        segments(nc, k, "dst_seg", k.dst_keys, k.NT, P, k.d_prev, k.d_next, k.d_whole)
        edge_columns(nc, k)
        rank_phase(nc, k, "rank_src", k.fields[:, :, 0], lambda t: k.fields[:, bass.ds(t, 1), 0], 1, src_keys, k.pos_i)

        node_pass(nc, k, 0, a["x"], tables=(h0, ends0))
        hold = Phase(nc, "soft0")
        score, power = hold.sb("score", [P, k.TC]), hold.sb("power", [P, k.TC])
        rows, most = hold.sb("rows", [P, B, P]), hold.sb("most", [P, B, P])
        zero = hold.sem("zero")
        with nc.Block() as block:
            @block.vector
            def _(dve):
                nc.vector.memset(score[:], 0.0).then_inc(zero, 1)
        score_pass(nc, k, "score0", 0, ends0, ends0, out=score)
        to_rows(nc, k, "rows0", score, rows)
        segment_reduce(nc, k, "max0", rows, k.d_prev, k.d_next, k.d_whole, "max", most)
        powers(nc, k, "pow0", rows, most, power)
        aggregate(nc, k, "agg0", agg, table=h0, weight=lambda t: columns(power, t), ones=True)
        hold.close()

        node_pass(nc, k, 1, a["x"], x_out=x1, agg=agg, table_in=h0, tables=(h1,))
        aggregate(nc, k, "agg1", agg, table=h1, weight=lambda t: k.fields[:, bass.ds(t, 1), 2])

        node_pass(nc, k, 2, x1, x_out=x2, agg=agg, tables=(from_src, to_dst, h2))
        score_pass(nc, k, "score2", 2, from_src, to_dst, put=scores)
        shares_by_source(nc, k, src_keys.rearrange("r o -> (r o)"), scores, shares)
        aggregate(nc, k, "agg2", agg, table=h2, alpha=shares)

        node_pass(nc, k, 3, x2, x_out=x3, agg=agg, tables=(h3,))
        hold = Phase(nc, "soft3")
        messages, head_scores = hold.sb("messages", [P, k.NT, 65]), hold.sb("head_scores", [P, k.NT, 4])
        score_pass(nc, k, "score3", 3, h3, out=head_scores, messages=messages)
        head_powers(nc, k, head_scores, messages)
        aggregate(nc, k, "agg3", agg, heads=(
            lambda t: messages[:, bass.ds(t, 1), :].rearrange("p o f -> p (o f)"),
            lambda t: head_scores[:, bass.ds(t, 1), :].rearrange("p o f -> p (o f)")))
        hold.close()
        node_pass(nc, k, 4, x3, x_out=out, agg=agg)


_INS = ["x", "src", "dst", "edge_attr_2", "edge_weight", "L0_gnn_W", "L0_gnn_b", "L0_gnn_mag_w", "L0_gnn_mag_b",
        "L0_gnn_attn_w", "L1_gnn_w_nbr", "L1_gnn_w_own", "L1_gnn_bias", "L2_gnn_W_s", "L2_gnn_W_t", "L2_gnn_W_attn",
        "L2_gnn_W_fc", "L2_gnn_b_fc", "L3_gnn_W_forward", "L3_gnn_W_reverse", "L3_gnn_attn_forward"]


def kernel(**inputs):
    import numpy as np
    import concourse.bacc as bacc
    from concourse.bass_utils import run_bass_kernel_spmd

    nc = bacc.Bacc("TRN2", target_bir_lowering=False, num_devices=1)
    arrays, aps = {}, {}
    for name in _INS:
        array = np.ascontiguousarray(inputs[name])
        arrays[f"in_{name}"] = array
        aps[name] = nc.dram_tensor(f"in_{name}", array.shape, mybir.dt.from_np(array.dtype), kind="ExternalInput").ap()
    out = nc.dram_tensor("out_0", arrays["in_x"].shape, F32, kind="ExternalOutput").ap()
    gnn_kernel(nc, aps, out)
    result = run_bass_kernel_spmd(nc, [arrays], core_ids=[0])
    return result.results[0]["out_0"]
```

```python
from contextlib import ExitStack, nullcontext

import concourse.bass as bass
from concourse import mybir

ALU = mybir.AluOpType
ACT = mybir.ActivationFunctionType
AX = mybir.AxisListType
F32 = mybir.dt.float32
BF16 = mybir.dt.bfloat16
I32 = mybir.dt.int32

P = 128
U = 8
D = 256
AGG_W = 260
FAR = 1e30


class Phase:

    def __init__(self, nc, name):
        self.nc, self.name, self.sems, self.ctx = nc, name, [], ExitStack()

    def sb(self, name, shape, dt=F32):
        return self.ctx.enter_context(self.nc.sbuf_tensor(f"{self.name}_{name}", shape, dt))

    def ps(self, name, shape, dt=F32):
        return self.ctx.enter_context(self.nc.psum_tensor(f"{self.name}_{name}", shape, dt))

    def sem(self, name):
        self.sems.append(self.nc.alloc_semaphore(f"{self.name}_{name}"))
        return self.sems[-1]

    def sem_per_slot(self, name, n=U):
        return [self.sem(f"{name}{j}") for j in range(n)]

    def close(self):
        self.nc.clear_and_free_semaphores(self.sems)
        self.nc.all_engine_barrier()
        self.ctx.close()


def peeled(engine, count, body):
    body(0, True)
    if count > 1:
        with engine.Fori(1, count) as i:
            body(i, False)


class Chain:

    def __init__(self, engine, sem):
        self.engine, self.sem, self.n = engine, sem, 0

    def __call__(self, instruction):
        self.n += 1
        instruction.then_inc(self.sem, 1)
        self.engine.wait_ge(self.sem, self.n)


def columns(t, c, n=1):
    return t[:, bass.ds(c, n)]


def constants(nc, k):
    ph = Phase(nc, "const")
    filled, s_done = ph.sem("filled"), ph.sem("done")
    with nc.Block() as block:
        @block.gpsimd
        def _(pool):
            nc.gpsimd.memset(k.ones[:], 1.0).then_inc(filled, 1)
            nc.gpsimd.iota(k.ramp_i[:], pattern=[[1, k.TC]], base=0, channel_multiplier=0).then_inc(filled, 1)
            pool.wait_ge(filled, 2)
            nc.gpsimd.affine_select(out=k.ident[:], in_=k.ones[:], compare_op=ALU.is_equal, fill=0.0, base=0,
                                    pattern=[[-1, P]], channel_multiplier=1).then_inc(s_done, 1)
            nc.gpsimd.affine_select(out=k.before[:], in_=k.ones[:], compare_op=ALU.is_gt, fill=0.0, base=0,
                                    pattern=[[1, P]], channel_multiplier=-1).then_inc(s_done, 1)

        @block.vector
        def _(dve):
            nc.vector.memset(k.pos_i[:], 0).then_inc(s_done, 1)
            dve.wait_ge(filled, 2)
            nc.vector.tensor_copy(k.ramp[:], k.ramp_i[:]).then_inc(s_done, 1)
            dve.wait_ge(s_done, 4)
            nc.vector.tensor_copy(k.ident_bf[:], k.ident[:]).then_inc(s_done, 1)
    ph.close()


def load_edges(nc, k, a, rows):
    ph = Phase(nc, "load")
    E, TC, B = k.E, k.TC, k.TC // P
    raw_i = [ph.sb(f"raw_i{n}", [P, B, P], I32) for n in range(2)]
    raw = [ph.sb(f"raw{n}", [P, B, P]) for n in range(3)]
    pair = ph.sb("pair", [P, B, P, 2])
    row_form = ph.sb("row_form", [P, B, P, 5])
    prev_i, prev = ph.sb("prev_i", [P, B], I32), ph.sb("prev", [P, B])
    falls, most = ph.sb("falls", [P, B, P]), ph.sb("most", [P, 1])
    any_fall = ph.sb("any_fall", [1, 1])
    p_falls = ph.ps("p_falls", [P, 512])
    part = [ph.sb(f"part{n}", [P, B, P]) for n in range(2)]
    turned = [ph.ps(f"turned{n}", [P, B * P]) for n in range(5)]
    preset, landed, cast, turn, s_done = (ph.sem(n) for n in ("preset", "landed", "cast", "turn", "done"))
    step, summed, rows_made, rows_put = (ph.sem(n) for n in ("step", "summed", "rows_made", "rows_put"))
    full, rest = E // P, E % P

    def runs():
        for b in range(B):
            n = min(P, full - b * P)
            if n > 0:
                yield slice(0, n), b, slice(0, P), b * P * P, n, P
        if rest:
            yield slice(full % P, full % P + 1), full // P, slice(0, rest), full * P, 1, rest

    def before_runs():
        for b in range(B):
            lo, hi = max(1, b * P), min((b + 1) * P, -(-E // P))
            if hi > lo:
                yield slice(lo - b * P, hi - b * P), b, lo, hi

    n_landed = 64 * len(list(runs())) + 16 * len(list(before_runs()))
    with nc.Block() as block:
        @block.gpsimd
        def _(pool):
            nc.gpsimd.iota(prev_i[:], pattern=[[P * P, B]], base=-1, channel_multiplier=P).then_inc(preset, 1)
            for t in raw_i:
                nc.gpsimd.iota(t[:], pattern=[[P * P, B], [1, P]], base=0, channel_multiplier=P).then_inc(preset, 1)

        @block.sync
        def _(sp):
            sp.wait_ge(preset, 5)
            for at_rows, b, cols, at, n, w in runs():
                for field, t in ((a["src"], raw_i[0]), (a["dst"], raw_i[1]), (a["edge_weight"], raw[2])):
                    sp.dma_start(t[at_rows, b, cols], field[at:at + n * w].rearrange("(n w) -> n w", w=w)).then_inc(landed, 16)
                sp.dma_start(pair[at_rows, b, cols, :].rearrange("n w c -> n (w c)"),
                             a["edge_attr_2"][at:at + n * w, :].rearrange("(n w) c -> n (w c)", w=w)).then_inc(landed, 16)
            for at_rows, b, lo, hi in before_runs():
                sp.dma_start(prev_i[at_rows, b:b + 1],
                             a["dst"][(lo - 1) * P:(hi - 1) * P].rearrange("(n w) -> n w", w=P)[:, P - 1:P],
                             allow_slow_non_contiguous=True).then_inc(landed, 16)
            sp.wait_ge(rows_made, 5)
            for b in range(B):
                n = min(P, k.NT - b * P)
                sp.dma_start(rows[b * P * P:(b * P + n) * P, :].rearrange("(a p) f -> a (p f)", p=P),
                             row_form[0:n, b, :, :].rearrange("a p f -> a (p f)")).then_inc(rows_put, 16)
            sp.wait_ge(rows_put, 16 * B)

        @block.vector
        def _(dve):
            nc.vector.memset(raw[2][:], 0.0).then_inc(preset, 1)
            nc.vector.memset(pair[:], 0.0).then_inc(preset, 1)
            dve.wait_ge(landed, n_landed)
            for n in range(2):
                nc.vector.tensor_copy(raw[n][:], raw_i[n][:]).then_inc(cast, 1)
            for n in range(2):
                nc.vector.tensor_copy(part[n][:], pair[:, :, :, n]).then_inc(cast, 1)
            dve.wait_ge(cast, 4)
            for n, t in enumerate([raw[0], raw[1], raw[2], part[0], part[1]]):
                nc.vector.tensor_copy(row_form[:, :, :, n], t[:]).then_inc(rows_made, 1)
            chain = Chain(dve, step)
            chain(nc.vector.tensor_copy(prev[:], prev_i[:]))
            chain(nc.vector.tensor_tensor(falls[:, :, 0], prev[:], raw[1][:, :, 0], ALU.is_gt))
            chain(nc.vector.tensor_tensor(falls[:, :, 1:P], raw[1][:, :, 0:P - 1], raw[1][:, :, 1:P], ALU.is_gt))
            chain(nc.vector.tensor_reduce(most[:], falls[:].rearrange("p b q -> p (b q)"), AX.X, ALU.max))
            dve.wait_ge(summed, 1)
            chain(nc.vector.tensor_scalar(any_fall[:], p_falls[0:1, 0:1], 0.5, None, ALU.is_gt))
            chain(nc.vector.tensor_copy(k.unsorted[:], any_fall[:]))
            for n in range(5):
                dve.wait_ge(turn, n + 1)
                nc.vector.tensor_copy(k.fields[:, :, n], turned[n][:]).then_inc(s_done, 1)

        @block.tensor
        def _(pe):
            pe.wait_ge(cast, 4)
            pe.wait_ge(landed, n_landed)
            for n, t in enumerate([raw[0], raw[1], raw[2], part[0], part[1]]):
                for b in range(B):
                    ins = nc.tensor.transpose(turned[n][:, b * P:(b + 1) * P], t[:, b, :], k.ident[:])
                ins.then_inc(turn, 1)
            pe.wait_ge(step, 4)
            nc.tensor.matmul(p_falls[0:1, 0:1], most[:], k.ones[:, 0:1], start=True, stop=True).then_inc(summed, 1)
    ph.close()


def rank_phase(nc, k, name, key, payload=None, width=0, target=None, pos_out=None, only_if=None, beside=None):
    ph = Phase(nc, name)
    NI, NT, NTH = k.NT // U, k.NT, k.NT
    key_i, part_i = ph.sb("key_i", [P, k.TC], I32), ph.sb("part_i", [P, k.TC], I32)
    high, low = ph.sb("high", [P, k.TC]), ph.sb("low", [P, k.TC])
    at_high = [ph.sb(f"at_high{n}", [P, NTH], BF16) for n in range(U)]
    at_low = [ph.sb(f"at_low{n}", [P, P], BF16) for n in range(U)]
    low_t = [ph.sb(f"low_t{n}", [P, P]) for n in range(2)]
    low_tb = [ph.sb(f"low_tb{n}", [P, P], BF16) for n in range(2)]
    earlier = [ph.sb(f"earlier{n}", [P, P], BF16) for n in range(2)]
    starts = [ph.sb(f"starts{n}", [P, NTH]) for n in range(2)]
    counts, below, upto, zeros = (ph.sb(n, [P, NTH]) for n in ("counts", "below", "upto", "zeros"))
    picked = [ph.sb(f"picked{n}", [P, NTH], BF16) for n in range(2)]
    rank_f, rank_i = ph.sb("rank_f", [P, U]), ph.sb("rank_i", [P, U], I32)
    row = ph.sb("row", [P, U, width]) if target is not None else None
    p_turn = [ph.ps(f"turn{n}", [P, 1024], BF16) for n in range(2)]
    p_same = [ph.ps(f"same{n}", [P, 512]) for n in range(2)]
    p_count = p_same[0][:, 0:NTH]
    p_rank = [ph.ps(f"rank{n}", [P, 512]) for n in range(2)]
    p_add = [ph.ps(f"add{n}", [P, 512]) for n in range(2)]
    digits, hist_hot, hist_mm = ph.sem("digits"), ph.sem("hist_hot"), ph.sem("hist_mm")
    prefix, prefix_mm, low_hot, high_hot = ph.sem("prefix"), ph.sem("prefix_mm"), ph.sem("low_hot"), ph.sem("high_hot")
    turned, copied, same, masked = ph.sem("turned"), ph.sem("copied"), ph.sem("same"), ph.sem("masked")
    ranked, added, advanced, picked_n = ph.sem("ranked"), ph.sem("added"), ph.sem("advanced"), ph.sem("picked_n")
    index_ready, row_ready, turn_pool = ph.sem("index_ready"), ph.sem("row_ready"), ph.sem("turn_pool")
    stored = ph.sem_per_slot("stored") if target is not None else None
    if beside is not None:
        beside.open(ph)
    rank_kept = ph.sem("rank_kept")

    def engaged(engine):
        if only_if is None:
            return nullcontext()
        return engine.If(engine.value_load(only_if[0:1, 0:1], min_val=0, max_val=1) > 0)

    def hots(i, j, first, which, sem_low, sem_high, mm):
        t = i * U + j
        nc.vector.tensor_scalar(at_low[j][:], k.ramp[:, 0:P], columns(low, t), None, ALU.is_equal).then_inc(sem_low, 1)
        nc.vector.tensor_scalar(at_high[j][:], k.ramp[:, 0:NTH], columns(high, t), None, ALU.is_equal).then_inc(sem_high, 1)

    with nc.Block() as block:
        @block.vector
        def _(dve):
            with engaged(dve):
                chain = Chain(dve, digits)
                chain(nc.vector.memset(zeros[:], 0.0))
                chain(nc.vector.tensor_copy(key_i[:], key))
                chain(nc.vector.tensor_scalar(part_i[:], key_i[:], 7, None, ALU.logical_shift_right))
                chain(nc.vector.tensor_copy(high[:], part_i[:]))
                chain(nc.vector.tensor_scalar(part_i[:], key_i[:], P - 1, None, ALU.bitwise_and))
                chain(nc.vector.tensor_copy(low[:], part_i[:]))

                def histogram(i, first):
                    for j in range(U):
                        if not first:
                            dve.wait_ge(hist_mm, i * U + j - U + 1)
                        hots(i, j, first, 0, hist_hot, hist_hot, hist_mm)

                peeled(dve, NI, histogram)
                dve.wait_ge(hist_mm, NT)
                base = chain.n
                chain(nc.vector.tensor_copy(counts[:], p_count))
                dve.wait_ge(prefix_mm, 1)
                chain(nc.vector.tensor_copy(below[:], p_rank[0][:, 0:NTH]))
                chain(nc.vector.tensor_tensor_scan(upto[:], p_rank[1][:, 0:NTH], zeros[:], 0.0, ALU.add, ALU.add))
                chain(nc.vector.tensor_tensor(below[:], below[:], upto[:], ALU.add))
                chain(nc.vector.tensor_tensor(starts[0][:], below[:], p_rank[1][:, 0:NTH], ALU.subtract))
                dve.sem_inc(prefix, 1)

                def tiles(i, first):
                    for j in range(U):
                        t = i * U + j
                        if not first:
                            dve.wait_ge(ranked, t - U + 1)
                            dve.wait_ge(added, t - U + 1)
                            dve.wait_ge(picked_n, t - U + 1)
                        hots(i, j, first, 0, low_hot, high_hot, None)
                    for j in range(U):
                        t = i * U + j
                        dve.wait_ge(same, t + 1)
                        if not first or j >= 2:
                            dve.wait_ge(ranked, t - 1)
                        nc.vector.tensor_tensor(earlier[j % 2][:], p_same[j % 2][:, 0:P], k.before[:], ALU.mult).then_inc(masked, 1)
                        dve.wait_ge(added, t + 1)
                        if not first or j >= 1:
                            dve.wait_ge(ranked, t)
                            dve.wait_ge(advanced, t)
                        nc.vector.tensor_tensor(starts[(j + 1) % 2][:], starts[j % 2][:], p_add[j % 2][:, 0:NTH],
                                                ALU.add).then_inc(advanced, 1)
                        dve.wait_ge(ranked, t + 1)
                        dve.wait_ge(high_hot, t + 1)
                        if not first or j >= 2:
                            dve.wait_ge(picked_n, t - 1)
                        if not first:
                            dve.wait_ge(index_ready, t - U + 1)
                        nc.vector.tensor_tensor_reduce(picked[j % 2][:], at_high[j][:], p_rank[j % 2][:, 0:NTH], 1.0, 0.0,
                                                       ALU.mult, ALU.add, rank_f[:, j:j + 1]).then_inc(picked_n, 1)
                        dve.wait_ge(picked_n, t + 1)
                        if not first:
                            if target is not None:
                                dve.wait_ge(stored[j], i * 16)
                            else:
                                dve.wait_ge(rank_kept, i)
                        nc.vector.tensor_copy(rank_i[:, j:j + 1], rank_f[:, j:j + 1]).then_inc(index_ready, 1)
                        if beside is not None:
                            beside.vector(dve, i, j, first)
                    if pos_out is not None:
                        dve.wait_ge(index_ready, i * U + U)
                        nc.vector.tensor_copy(columns(pos_out, i * U, U), rank_i[:]).then_inc(rank_kept, 1)

                peeled(dve, NI, tiles)
                if beside is not None:
                    beside.vector_rest(dve)

        @block.tensor
        def _(pe):
            with engaged(pe):
                def histogram(i, first):
                    for j in range(U):
                        pe.wait_ge(hist_hot, (i * U + j + 1) * 2)
                        nc.tensor.matmul(p_count, at_low[j][:], at_high[j][:], start=first and j == 0, stop=False,
                                         skip_group_check=True).then_inc(hist_mm, 1)

                peeled(pe, NI, histogram)
                pe.wait_ge(digits, 7)
                nc.tensor.matmul(p_rank[0][:, 0:NTH], k.before[:], counts[:], start=True, stop=True)
                nc.tensor.matmul(p_rank[1][:, 0:NTH], k.ones[:], counts[:], start=True, stop=True).then_inc(prefix_mm, 1)

                def tiles(i, first):
                    def head(j):
                        t = i * U + j
                        pe.wait_ge(low_hot, t + 1)
                        if not first or j >= 2:
                            pe.wait_ge(copied, 2 * (t - 1))
                        nc.tensor.transpose(p_turn[j % 2][:, 0:P], at_low[j][:], k.ident_bf[:]).then_inc(turned, 1)

                    head(0)
                    for j in range(U):
                        t = i * U + j
                        if j + 1 < U:
                            head(j + 1)
                        pe.wait_ge(copied, 2 * (t + 1))
                        if not first or j >= 2:
                            pe.wait_ge(masked, t - 1)
                        nc.tensor.matmul(p_same[j % 2][:, 0:P], low_tb[j % 2][:], low_tb[j % 2][:], start=True,
                                         stop=True).then_inc(same, 1)
                        pe.wait_ge(high_hot, t + 1)
                        if first and j == 0:
                            pe.wait_ge(prefix, 1)
                        if not first or j >= 2:
                            pe.wait_ge(advanced, t - 1)
                        nc.tensor.matmul(p_add[j % 2][:, 0:NTH], at_low[j][:], at_high[j][:], start=True,
                                         stop=True).then_inc(added, 1)
                        if not first or j >= 2:
                            pe.wait_ge(picked_n, t - 1)
                        if not first or j >= 1:
                            pe.wait_ge(advanced, t)
                        nc.tensor.matmul(p_rank[j % 2][:, 0:NTH], low_t[j % 2][:], starts[j % 2][:], start=True, stop=False)
                        pe.wait_ge(masked, t + 1)
                        nc.tensor.matmul(p_rank[j % 2][:, 0:NTH], earlier[j % 2][:], at_high[j][:], start=False,
                                         stop=True).then_inc(ranked, 1)

                peeled(pe, NI, tiles)

        @block.scalar
        def _(act):
            with engaged(act):
                def tiles(i, first):
                    for j in range(U):
                        t = i * U + j
                        act.wait_ge(turned, t + 1)
                        if not first or j >= 2:
                            act.wait_ge(ranked, t - 1)
                            act.wait_ge(same, t - 1)
                        nc.scalar.copy(low_tb[j % 2][:], p_turn[j % 2][:, 0:P]).then_inc(copied, 1)
                        nc.scalar.copy(low_t[j % 2][:], p_turn[j % 2][:, 0:P]).then_inc(copied, 1)
                        if target is not None:
                            if not first:
                                act.wait_ge(stored[j], i * 16)
                            nc.scalar.copy(row[:, j, :], payload(t)).then_inc(row_ready, 1)
                        if beside is not None:
                            beside.scalar(act, i, j, first)

                if beside is not None:
                    beside.scalar_start(act)
                peeled(act, NI, tiles)

        @block.gpsimd
        def _(pool):
            with engaged(pool):
                def tiles(i, first):
                    for j in range(U):
                        t = i * U + j
                        if beside is not None:
                            beside.gpsimd(pool, i, j, first)
                        if target is not None:
                            pool.wait_ge(index_ready, t + 1)
                            pool.sem_inc(turn_pool, 1)
                            pool.wait_ge(row_ready, t + 1)
                            pool.sem_inc(turn_pool, 1)
                            nc.gpsimd.indirect_dma_start(target, bass.IndirectOffsetOnAxis(rank_i[:, j:j + 1], 0), row[:, j, :],
                                                         None, bounds_check=k.NP - 1, oob_is_err=False).then_inc(stored[j], 16)

                peeled(pool, NI, tiles)
                if target is not None:
                    for j in range(U):
                        pool.wait_ge(stored[j], NI * 16)
    ph.close()


class EndSums:
    LAG = 4

    def __init__(self, nc, k, ends, out):
        self.nc, self.k, self.ends, self.out = nc, k, ends, out

    def open(self, ph):
        self.of_src = [ph.sb(f"of_src{j}", [P, 2]) for j in range(U)]
        self.of_dst = [ph.sb(f"of_dst{j}", [P, 2]) for j in range(U)]
        self.take_src, self.take_dst = ph.sb("take_src", [P, U], I32), ph.sb("take_dst", [P, U], I32)
        self.indexed, self.turn, self.scored = ph.sem("indexed"), ph.sem("turn"), ph.sem("scored")
        self.src_got, self.dst_got = ph.sem_per_slot("src_got"), ph.sem_per_slot("dst_got")

    def index(self, act, t, j, late):
        if late is not None:
            act.wait_ge(self.src_got[j], 16 * late)
            act.wait_ge(self.dst_got[j], 16 * late)
        self.nc.scalar.copy(self.take_src[:, j:j + 1], columns(self.k.src_i, t)).then_inc(self.indexed, 1)
        self.nc.scalar.copy(self.take_dst[:, j:j + 1], columns(self.k.dst_i, t)).then_inc(self.indexed, 1)

    def scalar_start(self, act):
        for j in range(self.LAG):
            self.index(act, j, j, None)

    def scalar(self, act, i, j, first):
        t = i * U + j
        if j < U - self.LAG:
            self.index(act, t + self.LAG, j + self.LAG, None if first else i)
        else:
            self.index(act, t + self.LAG, j + self.LAG - U, i + 1)

    def gpsimd(self, pool, i, j, first):
        t = i * U + j
        pool.wait_ge(self.indexed, 2 * (t + 1))
        pool.sem_inc(self.turn, 1)
        if not first:
            pool.wait_ge(self.scored, t - U + 1)
            pool.sem_inc(self.turn, 1)
        self.nc.gpsimd.indirect_dma_start(self.of_src[j][:], None, self.ends,
                                          bass.IndirectOffsetOnAxis(self.take_src[:, j:j + 1], 0)).then_inc(self.src_got[j], 16)
        self.nc.gpsimd.indirect_dma_start(self.of_dst[j][:], None, self.ends,
                                          bass.IndirectOffsetOnAxis(self.take_dst[:, j:j + 1], 0)).then_inc(self.dst_got[j], 16)

    def add(self, dve, t, j, uses):
        dve.wait_ge(self.src_got[j], 16 * uses)
        dve.wait_ge(self.dst_got[j], 16 * uses)
        self.nc.vector.tensor_tensor(columns(self.out, t), self.of_src[j][:, 0:1], self.of_dst[j][:, 1:2],
                                     ALU.add).then_inc(self.scored, 1)

    def vector(self, dve, i, j, first):
        if j >= self.LAG:
            self.add(dve, i * U + j - self.LAG, j - self.LAG, i + 1)
        elif not first:
            self.add(dve, i * U + j - self.LAG, j - self.LAG + U, i)

    def vector_rest(self, dve):
        NI = self.k.NT // U
        for j in range(U - self.LAG, U):
            self.add(dve, (NI - 1) * U + j, j, NI)
def segments(nc, k, name, keys, rows, width, same_prev, same_next, whole, field=0):
    ph = Phase(nc, name)
    B = whole.shape[1]
    fields = keys.shape[1]
    got = ph.sb("got", [P, B, width, fields])
    key = got[:, :, :, field]
    prev, nxt = ph.sb("prev", [P, B]), ph.sb("next", [P, B])
    preset, landed, s_done = ph.sem("preset"), ph.sem("landed"), ph.sem("done")
    table = keys.rearrange("(r w) c -> r w c", w=width)
    n_dma = 0
    for b in range(B):
        n = min(P, rows - b * P)
        n_dma += 1 + (n - (b == 0) > 0) + (min(n, rows - b * P - 1) > 0)
    with nc.Block() as block:
        @block.sync
        def _(sp):
            sp.wait_ge(preset, 3)
            for b in range(B):
                r, n = b * P, min(P, rows - b * P)
                sp.dma_start(got[0:n, b, :, :].rearrange("r w c -> r (w c)"),
                             table[r:r + n, :, :].rearrange("r w c -> r (w c)")).then_inc(landed, 16)
                a = 1 if b == 0 else 0
                if n > a:
                    sp.dma_start(prev[a:n, b:b + 1], table[r + a - 1:r + n - 1, width - 1, field:field + 1],
                                 allow_slow_non_contiguous=True).then_inc(landed, 16)
                m = min(n, rows - r - 1)
                if m > 0:
                    sp.dma_start(nxt[0:m, b:b + 1], table[r + 1:r + 1 + m, 0, field:field + 1],
                                 allow_slow_non_contiguous=True).then_inc(landed, 16)

        @block.vector
        def _(dve):
            nc.vector.memset(got[:], -5.0).then_inc(preset, 1)
            nc.vector.memset(prev[:], -1.0).then_inc(preset, 1)
            nc.vector.memset(nxt[:], -2.0).then_inc(preset, 1)
            dve.wait_ge(landed, 16 * n_dma)
            last = width - 1
            for out, a0, a1 in ((same_prev[:, :, 1:width], key[:, :, 1:width], key[:, :, 0:last]),
                                (same_prev[:, :, 0], key[:, :, 0], prev[:]),
                                (same_next[:, :, 0:last], key[:, :, 0:last], key[:, :, 1:width]),
                                (same_next[:, :, last], key[:, :, last], nxt[:]),
                                (whole[:], key[:, :, 0], key[:, :, last])):
                nc.vector.tensor_tensor(out, a0, a1, ALU.is_equal).then_inc(s_done, 1)
    ph.close()


def segment_reduce(nc, k, name, val, same_prev, same_next, whole, op, out):
    ph = Phase(nc, name)
    B, W = whole.shape[1], val.shape[2]
    most = op == "max"
    none = -FAR if most else 0.0
    step, join = (ALU.add, ALU.max) if most else (ALU.mult, ALU.add)
    go_f, go_b, go_w = ph.sb("go_f", [P, B, W]), ph.sb("go_b", [P, B, W]), ph.sb("go_w", [P, B])
    fwd, bwd = ph.sb("fwd", [P, B, W]), ph.sb("bwd", [P, B, W])
    ends = ph.sb("ends", [P, 6, B])
    rows = ph.sb("rows", [1, 6, B * P])
    total = ph.sb("total", [1, 2, B * P])
    carry_row = ph.sb("carry_row", [1, 2, B * P])
    carry = ph.sb("carry", [P, 2, B])
    p_rows = [ph.ps(f"rows{n}", [P, 512]) for n in range(6)]
    p_carry = ph.ps("p_carry", [P, 512])
    step_done, ends_out, rows_in = ph.sem("step"), ph.sem("ends_out"), ph.sem("rows_in")
    F, L = slice(0, W), W - 1

    def scans(chain, init_f, init_b):
        for b in range(B):
            nc.vector.tensor_tensor_scan(fwd[:, b, :], go_f[:, b, :], val[:, b, :], init_f(b), step, join)
            ins = nc.vector.tensor_tensor_scan(bwd[:, b, ::-1], go_b[:, b, ::-1], val[:, b, ::-1], init_b(b), step, join)
            chain(ins)

    with nc.Block() as block:
        @block.vector
        def _(dve):
            chain = Chain(dve, step_done)
            for t, s in ((go_f, same_prev), (go_b, same_next), (go_w, whole)):
                if most:
                    chain(nc.vector.tensor_scalar(t[:], s[:], -1.0, FAR, ALU.add, ALU.mult))
                else:
                    chain(nc.vector.tensor_copy(t[:], s[:]))
            scans(chain, lambda b: none, lambda b: none)
            chain(nc.vector.tensor_copy(ends[:, 0, :], fwd[:, :, L]))
            chain(nc.vector.tensor_copy(ends[:, 3, :], bwd[:, :, 0]))
            chain(nc.vector.tensor_tensor(ends[:, 1, :], go_f[:, :, 0], go_w[:], step))
            chain(nc.vector.tensor_tensor(ends[:, 4, :], go_b[:, :, L], go_w[:], step))
            chain(nc.vector.tensor_copy(ends[:, 2, :], go_f[:, :, 0]))
            chain(nc.vector.tensor_copy(ends[:, 5, :], go_b[:, :, L]))
            dve.sem_inc(ends_out, 1)
            dve.wait_ge(rows_in, 1)
            for n in range(6):
                chain(nc.vector.tensor_copy(rows[:, n, :], p_rows[n][0:1, 0:B * P]))
            chain(nc.vector.tensor_tensor_scan(total[:, 0, :], rows[:, 1, :], rows[:, 0, :], none, step, join))
            chain(nc.vector.tensor_tensor_scan(total[:, 1, ::-1], rows[:, 4, ::-1], rows[:, 3, ::-1], none, step, join))
            chain(nc.vector.memset(carry_row[:], none))
            n = B * P
            chain(nc.vector.tensor_tensor(carry_row[:, 0, 1:n], rows[:, 2, 1:n], total[:, 0, 0:n - 1], step))
            chain(nc.vector.tensor_tensor(carry_row[:, 1, 0:n - 1], rows[:, 5, 0:n - 1], total[:, 1, 1:n], step))
            dve.sem_inc(ends_out, 1)
            dve.wait_ge(rows_in, 2)
            chain(nc.vector.tensor_copy(carry[:].rearrange("p s b -> p (s b)"), p_carry[:, 0:2 * B]))
            scans(chain, lambda b: carry[:, 0, b:b + 1], lambda b: carry[:, 1, b:b + 1])
            if most:
                chain(nc.vector.tensor_tensor(out[:], fwd[:], bwd[:], ALU.max))
            else:
                chain(nc.vector.tensor_tensor(out[:], fwd[:], bwd[:], ALU.add))
                chain(nc.vector.tensor_tensor(out[:], out[:], val[:], ALU.subtract))

        @block.tensor
        def _(pe):
            pe.wait_ge(ends_out, 1)
            for n in range(6):
                for b in range(B):
                    ins = nc.tensor.transpose(p_rows[n][0:1, b * P:(b + 1) * P], ends[:, n, b:b + 1], k.ident[:])
            ins.then_inc(rows_in, 1)
            pe.wait_ge(ends_out, 2)
            for s in range(2):
                for b in range(B):
                    ins = nc.tensor.transpose(p_carry[:, s * B + b:s * B + b + 1], carry_row[0:1, s, b * P:(b + 1) * P],
                                              k.ident[0:1, 0:1])
            ins.then_inc(rows_in, 1)
    ph.close()


def sorted_edges(nc, k, sorted_rows, dst_keys):
    ph = Phase(nc, "sorted")
    B, NT = k.TC // P, k.NT
    got = ph.sb("got", [P, B, P, 5])
    field = [ph.sb(f"field{n}", [P, B, P]) for n in range(5)]
    turned = [ph.ps(f"turned{n}", [P, B * P]) for n in range(5)]
    preset, landed, split, turn, s_done, kept = (ph.sem(n) for n in ("preset", "landed", "split", "turn", "done", "kept"))
    with nc.Block() as block:
        @block.sync
        def _(sp):
            sp.wait_ge(preset, 1)
            for b in range(B):
                n = min(P, NT - b * P)
                sp.dma_start(got[0:n, b, :, :].rearrange("a p f -> a (p f)"),
                             sorted_rows[b * P * P:(b * P + n) * P, :].rearrange("(a p) f -> a (p f)", p=P)).then_inc(landed, 16)
            sp.wait_ge(split, 5)
            for b in range(B):
                n = min(P, NT - b * P)
                sp.dma_start(dst_keys[b * P * P:(b * P + n) * P].rearrange("(a p) -> a p", p=P),
                             field[1][0:n, b, :]).then_inc(kept, 16)
            sp.wait_ge(kept, 16 * B)

        @block.vector
        def _(dve):
            nc.vector.memset(got[:], 0.0).then_inc(preset, 1)
            dve.wait_ge(landed, 16 * B)
            for n in range(5):
                nc.vector.tensor_copy(field[n][:], got[:, :, :, n]).then_inc(split, 1)
            for n in range(5):
                dve.wait_ge(turn, n + 1)
                nc.vector.tensor_copy(k.fields[:, :, n], turned[n][:]).then_inc(s_done, 1)

        @block.tensor
        def _(pe):
            for n in range(5):
                pe.wait_ge(split, n + 1)
                for b in range(B):
                    ins = nc.tensor.transpose(turned[n][:, b * P:(b + 1) * P], field[n][:, b, :], k.ident[:])
                ins.then_inc(turn, 1)
    ph.close()


def edge_columns(nc, k):
    ph = Phase(nc, "columns")
    TC = k.TC
    tmp = ph.sb("tmp", [P, TC])
    bottom = ph.sb("bottom", [P, 1])
    step = ph.sem("step")
    with nc.Block() as block:
        @block.vector
        def _(dve):
            chain = Chain(dve, step)
            chain(nc.vector.tensor_copy(k.src_i[:], k.fields[:, :, 0]))
            chain(nc.vector.tensor_copy(k.dst_i[:], k.fields[:, :, 1]))
            chain(nc.vector.memset(k.dst_before[:], -1.0))
            chain(nc.vector.tensor_copy(bottom[:], k.ident[:, P - 1:P]))
            chain(nc.vector.tensor_scalar(tmp[:], k.fields[:, :, 1], 1.0, None, ALU.add))
            chain(nc.vector.tensor_scalar(k.dst_before[:, 1:TC], tmp[:, 0:TC - 1], bottom[:], -1.0, ALU.mult, ALU.add))
    ph.close()


def last_places(nc, k, sums, places):
    ph = Phase(nc, "places")
    NT, NI, B = k.NT, k.NT // U, k.TC // P
    key_i, part_i = ph.sb("key_i", [P, k.TC], I32), ph.sb("part_i", [P, k.TC], I32)
    high, low = ph.sb("high", [P, k.TC]), ph.sb("low", [P, k.TC])
    at_high = [ph.sb(f"at_high{n}", [P, NT], BF16) for n in range(U)]
    at_low = [ph.sb(f"at_low{n}", [P, P], BF16) for n in range(U)]
    counts, upto, zeros, within = (ph.sb(n, [P, NT]) for n in ("counts", "upto", "zeros", "within"))
    zero_row = ph.sb("zero_row", [1, AGG_W])
    reached, place = ph.sb("reached", [P, NT]), ph.sb("place", [P, k.TC])
    rows_i = ph.sb("rows_i", [P, B, P], I32)
    p_count, p_within, p_all = (ph.ps(n, [P, 512]) for n in ("p_count", "p_within", "p_all"))
    p_turn = ph.ps("p_turn", [P, k.TC])
    step, hot, counted, summed, turned, rows_made, stored = (
        ph.sem(n) for n in ("step", "hot", "counted", "summed", "turned", "rows_made", "stored"))

    with nc.Block() as block:
        @block.vector
        def _(dve):
            chain = Chain(dve, step)
            chain(nc.vector.memset(zeros[:], 0.0))
            chain(nc.vector.memset(place[:], 0.0))
            chain(nc.vector.memset(zero_row[:], 0.0))
            chain(nc.vector.tensor_copy(key_i[:], k.fields[:, :, 1]))
            chain(nc.vector.tensor_scalar(part_i[:], key_i[:], 7, None, ALU.logical_shift_right))
            chain(nc.vector.tensor_copy(high[:], part_i[:]))
            chain(nc.vector.tensor_scalar(part_i[:], key_i[:], P - 1, None, ALU.bitwise_and))
            chain(nc.vector.tensor_copy(low[:], part_i[:]))

            def tiles(i, first):
                for j in range(U):
                    t = i * U + j
                    if not first:
                        dve.wait_ge(counted, t - U + 1)
                    nc.vector.tensor_scalar(at_low[j][:], k.ramp[:, 0:P], columns(low, t), None, ALU.is_equal)
                    nc.vector.tensor_scalar(at_high[j][:], k.ramp[:, 0:NT], columns(high, t), None,
                                            ALU.is_equal).then_inc(hot, 1)
            peeled(dve, NI, tiles)
            dve.wait_ge(counted, NT)
            chain(nc.vector.tensor_copy(counts[:], p_count[:, 0:NT]))
            dve.wait_ge(summed, 1)
            chain(nc.vector.tensor_tensor_scan(upto[:], p_all[:, 0:NT], zeros[:], 0.0, ALU.add, ALU.add))
            chain(nc.vector.tensor_tensor(upto[:], upto[:], p_all[:, 0:NT], ALU.subtract))
            chain(nc.vector.tensor_tensor(within[:], p_within[:, 0:NT], counts[:], ALU.add))
            chain(nc.vector.tensor_tensor(within[:], within[:], upto[:], ALU.add))
            chain(nc.vector.tensor_scalar(reached[:], counts[:], 0.5, None, ALU.is_gt))
            chain(nc.vector.tensor_scalar(within[:], within[:], float(-1 - k.NP), None, ALU.add))
            chain(nc.vector.tensor_tensor(within[:], within[:], reached[:], ALU.mult))
            chain(nc.vector.tensor_scalar(place[:, 0:NT], within[:], float(k.NP), None, ALU.add))
            dve.wait_ge(turned, 1)
            nc.vector.tensor_copy(rows_i[:].rearrange("p b q -> p (b q)"), p_turn[:]).then_inc(rows_made, 1)

        @block.tensor
        def _(pe):
            def tiles(i, first):
                for j in range(U):
                    pe.wait_ge(hot, i * U + j + 1)
                    nc.tensor.matmul(p_count[:, 0:NT], at_low[j][:], at_high[j][:], start=first and j == 0, stop=False,
                                     skip_group_check=True).then_inc(counted, 1)
            peeled(pe, NI, tiles)
            pe.wait_ge(step, 9)
            nc.tensor.matmul(p_within[:, 0:NT], k.before[:], counts[:], start=True, stop=True)
            nc.tensor.matmul(p_all[:, 0:NT], k.ones[:], counts[:], start=True, stop=True).then_inc(summed, 1)
            pe.wait_ge(step, 17)
            for b in range(B):
                ins = nc.tensor.transpose(p_turn[:, b * P:(b + 1) * P], place[:, b * P:(b + 1) * P], k.ident[:])
            ins.then_inc(turned, 1)

        @block.sync
        def _(sp):
            sp.wait_ge(step, 3)
            sp.dma_start(sums[k.NP:k.NP + 1, :], zero_row[:]).then_inc(stored, 16)
            sp.wait_ge(rows_made, 1)
            for b in range(B):
                n = min(P, NT - b * P)
                sp.dma_start(places[b * P * P:(b * P + n) * P].rearrange("(a p) -> a p", p=P),
                             rows_i[0:n, b, :]).then_inc(stored, 16)
            sp.wait_ge(stored, 16 * (B + 1))
    ph.close()


def aggregate(nc, k, name, agg, table=None, weight=None, ones=False, alpha=None, heads=None):
    ph = Phase(nc, name)
    NI, LAG = k.NT // U, 4
    HALF = U // 2
    STORE_LAG = 5
    assert NI > 1
    width = AGG_W
    cols = AGG_W if heads else (D + 1 if ones else D)
    dst_row = ph.sb("dst_row", [P, U, P])
    rows = ph.sb("rows", [P, U, cols])
    mix = [ph.sb(f"mix{j}", [P, P]) for j in range(U)]
    hand_on = [ph.sb(f"hand_on{j}", [P, P]) for j in range(U)]
    total = ph.sb("total", [P, U, width])
    take_i, pos_i = (ph.sb(n, [P, U], I32) for n in ("take_i", "pos_i"))
    share = ph.sb("share", [P, U])
    p_sum = [ph.ps(f"sum{n}", [P, 512]) for n in range(4)]
    preset, mixed, summed, kept = ph.sem("preset"), ph.sem("mixed"), ph.sem("summed"), ph.sem("kept")
    indexed, turn_pool, turn_sp = ph.sem("indexed"), ph.sem("turn_pool"), ph.sem("turn_sp")
    row_in, taken, put = ph.sem_per_slot("row_in", U // HALF), ph.sem_per_slot("taken"), ph.sem_per_slot("put")
    share_in = ph.sem_per_slot("share_in") if alpha is not None else None
    keys = k.dst_keys
    n_preset = 1 + bool(ones)

    with nc.Block() as block:
        @block.sync
        def _(sp):
            def store(t, j):
                sp.wait_ge(kept, t + 1)
                sp.sem_inc(turn_sp, 1)
                sp.dma_start(agg[bass.ds(t * P, P), :], total[:, j, :]).then_inc(put[j], 16)

            def tiles(i, first):
                for j in range(U):
                    t = i * U + j
                    if j % HALF == 0:
                        if not first:
                            sp.wait_ge(mixed, t - U + HALF)
                            sp.sem_inc(turn_sp, 1)
                        sp.dma_start(dst_row[:, j:j + HALF, :].rearrange("p t q -> p (t q)"),
                                     keys[bass.ds(t * P, HALF * P)].rearrange("(a q) -> a q", a=1)
                                     .to_broadcast([P, HALF * P])).then_inc(row_in[j // HALF], 16)
                    if not first or j >= STORE_LAG:
                        store(t - STORE_LAG, (j - STORE_LAG) % U)
            peeled(sp, NI, tiles)
            for j in range(U - STORE_LAG, U):
                store((NI - 1) * U + j, j)
            for j in range(U):
                sp.wait_ge(put[j], 16 * NI)

        @block.vector
        def _(dve):
            nc.vector.memset(total[:], 0.0).then_inc(preset, 1)
            if ones:
                nc.vector.memset(rows[:, :, D:D + 1], 1.0).then_inc(preset, 1)

            def tiles(i, first):
                for j in range(U):
                    t = i * U + j
                    dve.wait_ge(row_in[j // HALF], 16 * (i + 1))
                    if not first:
                        dve.wait_ge(summed, t - U + 1)
                    if alpha is not None:
                        dve.wait_ge(share_in[j], 16 * (i + 1))
                    if heads:
                        nc.vector.tensor_scalar(mix[j][:], dst_row[:, j, :], k.dst_f(t), None, ALU.is_equal)
                        message, power = heads
                        nc.vector.tensor_tensor(
                            rows[:, j, :].rearrange("p (h f) -> p h f", h=4),
                            message(t).rearrange("p (o f) -> p o f", o=1).to_broadcast([P, 4, 65]),
                            power(t).rearrange("p (h o) -> p h o", o=1).to_broadcast([P, 4, 65]), ALU.mult)
                    else:
                        w = share[:, j:j + 1] if alpha is not None else weight(t)
                        nc.vector.tensor_scalar(mix[j][:], dst_row[:, j, :], k.dst_f(t), w, ALU.is_equal, ALU.mult)
                    nc.vector.tensor_scalar(hand_on[j][:], dst_row[:, j, :], columns(k.dst_before, t), None,
                                            ALU.is_equal).then_inc(mixed, 1)
            peeled(dve, NI, tiles)

        @block.tensor
        def _(pe):
            def tiles(i, first):
                for j in range(U):
                    t = i * U + j
                    pe.wait_ge(mixed, t + 1)
                    if table is not None:
                        pe.wait_ge(taken[j], 16 * (i + 1))
                    if first and j == 0:
                        pe.wait_ge(preset, n_preset)
                    if not first or j >= 4:
                        pe.wait_ge(kept, t - 3)
                    alone = first and j == 0
                    ins = nc.tensor.matmul(p_sum[j % 4][:, 0:cols], mix[j][:], rows[:, j, :], start=True, stop=alone)
                    if not alone:
                        pe.wait_ge(kept, t)
                        ins = nc.tensor.matmul(p_sum[j % 4][:, 0:cols], hand_on[j][:], total[:, (j - 1) % U, 0:cols],
                                               start=False, stop=True)
                    ins.then_inc(summed, 1)
            peeled(pe, NI, tiles)

        @block.scalar
        def _(act):
            def index(t, j, late):
                if late is not None and table is not None:
                    act.wait_ge(taken[j], 16 * late)
                if late is not None and alpha is not None:
                    act.wait_ge(share_in[j], 16 * late)
                if alpha is not None:
                    nc.scalar.copy(pos_i[:, j:j + 1], columns(k.pos_i, t))
                nc.scalar.copy(take_i[:, j:j + 1], columns(k.src_i, t)).then_inc(indexed, 1)

            for j in range(LAG):
                index(j, j, None)
            act.wait_ge(preset, n_preset)

            def tiles(i, first):
                for j in range(U):
                    t = i * U + j
                    act.wait_ge(summed, t + 1)
                    if not first:
                        act.wait_ge(put[j], 16 * i)
                    nc.scalar.copy(total[:, j, 0:cols], p_sum[j % 4][:, 0:cols]).then_inc(kept, 1)
                    if j < U - LAG:
                        index(t + LAG, j + LAG, None if first else i)
                    else:
                        index(t + LAG, j + LAG - U, i + 1)
            peeled(act, NI, tiles)

        @block.gpsimd
        def _(pool):
            def tiles(i, first):
                for j in range(U):
                    t = i * U + j
                    pool.wait_ge(indexed, t + 1)
                    pool.sem_inc(turn_pool, 1)
                    if alpha is not None:
                        if not first:
                            pool.wait_ge(mixed, t - U + 1)
                            pool.sem_inc(turn_pool, 1)
                        nc.gpsimd.indirect_dma_start(share[:, j:j + 1], None, alpha,
                                                     bass.IndirectOffsetOnAxis(pos_i[:, j:j + 1], 0)).then_inc(share_in[j], 16)
                    if table is not None:
                        if not first:
                            pool.wait_ge(summed, t - U + 1)
                            pool.sem_inc(turn_pool, 1)
                        nc.gpsimd.indirect_dma_start(rows[:, j, 0:D], None, table,
                                                     bass.IndirectOffsetOnAxis(take_i[:, j:j + 1], 0)).then_inc(taken[j], 16)
            if table is not None or alpha is not None:
                peeled(pool, NI, tiles)
    ph.close()
G = 4
ROWS = G * P


class Steps(Chain):

    def __init__(self, engine, sem, turn, each):
        self.engine, self.sem, self.base, self.n, self.each = engine, sem, turn * each, 0, each

    def __call__(self, instruction):
        self.n += 1
        assert self.n <= self.each
        instruction.then_inc(self.sem, 1)
        self.engine.wait_ge(self.sem, self.base + self.n)

    def end(self):
        assert self.n == self.each, (self.n, self.each)


def group_rows(table, base, n=ROWS):
    return table[bass.ds(base, n), :].rearrange("(p g) f -> p g f", g=G)


def spread(column, n):
    return column.rearrange("p (g o) -> p g o", o=1).to_broadcast([P, G, n])


GATHER_LAG = 2
S = 4


class Group:

    def __init__(self, H, side, uses, groups):
        self.H, self.h, self.i, self.groups = H, side, uses, groups
        self.new = isinstance(H, int) and H < S
        self.last = H - S + 1
        self.first, self.final = (isinstance(H, int) and H == at for at in (0, groups - 1))

    def next(self):
        return Group(self.H + 1, (self.h + 1) % S, self.i + (self.h + 1) // S, self.groups)


def uses_of(side, groups):
    return -(-(groups - side) // S)


def pipeline(engine, groups, stages, last_apart=False):
    deepest = max(lag for lag, _ in stages)
    looped = (groups - 2 * last_apart) // S
    peel = min(looped, -(-(deepest + S) // S))

    def step(i, c):
        for lag, stage in stages:
            side = (c - lag) % S
            uses = i + (c - lag - side) // S
            H = uses * S + side
            if isinstance(H, int) and not 0 <= H < groups:
                continue
            stage(Group(H, side, uses, groups))

    for s in range(S * peel):
        step(s // S, s % S)
    if looped > peel:
        with engine.Fori(peel, looped) as i:
            for c in range(S):
                step(i, c)
    for s in range(S * looped, groups + deepest):
        step(s // S, s % S)


def node_pass(nc, k, layer, x_in, x_out=None, agg=None, table_in=None, tables=()):
    ph = Phase(nc, f"node{layer}")
    groups = k.NT // G
    last_l = layer == 4
    n_put = {0: 2, 1: 2, 2: 3, 3: 1, 4: 0}[layer]
    n_out = {0: D + 3, 1: 2 * D, 2: 3 * D, 3: P + 8, 4: 0}[layer]
    banks = 2 if layer == 2 else 4

    def both(name, shape):
        return [ph.sb(f"{name}{h}", shape) for h in range(S)]

    x = both("x", [P, G, D])
    if layer:
        sums, xc = both("sums", [P, G, AGG_W]), both("xc", [P, G, D])
        place = [ph.sb(f"place{h}", [P, G], I32) for h in range(S)]
    if layer == 1:
        own_h, mixed = both("own_h", [P, G, D]), both("mixed", [P, G, D])
        small = [[ph.sb(f"small{h}_{n}", [P, G]) for n in range(12)] for h in range(S)]
        half = ph.sb("half", [P, G])
    if layer in (1, 4):
        den, inv = both("den", [P, G, 4]), both("inv", [P, G, 4])
    if last_l:
        scaled = both("scaled", [P, G, D])
    if layer in (2, 3):
        plain = both("plain", [P, G, D])
    if not last_l:
        xn = both("xn", [P, G, D])
        stats, moments = both("stats", [P, G, 6]), both("moments", [P, G, 2])
        var, inv_std = both("var", [P, G]), both("inv_std", [P, G])
        minus_half = ph.sb("minus_half", [P, G])
        h_t = [ph.sb(f"h_t{n}", [P, D]) for n in range(G)]
        out = both("out", [P, G, n_out])
        junk = [ph.sb(f"junk{n}", [P, D]) for n in range(2)]
        p_turn = [ph.ps(f"p_turn{n}", [P, 512]) for n in range(2)]
        p_out = [[ph.ps(f"p_out{w}_{n}", [P, 512]) for n in range(banks)] for w in range(len(k.products[layer]))]
    if layer == 0:
        size2, gate, size2m, inv_size, scale = (both(n, [P, G]) for n in ("size2", "gate", "size2m", "inv_size", "scale"))
        rows_h, pair_h = both("rows_h", [P, G, D]), both("pair_h", [P, G, 2])
    preset, joining, averaging = ph.sem("preset"), ph.sem("joining"), ph.sem("averaging")
    x_got, x_put, sums_got, own_got, t_put, place_got = (
        ph.sem_per_slot(n, S) for n in ("x_got", "x_put", "sums_got", "own_got", "t_put", "place_got"))
    joined, mixed_n, squared, factored, tanhed, pooling = (
        ph.sem(n) for n in ("joined", "mixed", "squared", "factored", "tanhed", "pooling"))
    var_made, std_made, normed, turned, rectified = (ph.sem(n) for n in ("var_made", "std_made", "normed", "turned", "rectified"))
    product, out_made, gated, scale_made, stats_in, raw_made, clamped, turn_pool, turn_sp, inverted = (
        ph.sem(n) for n in ("product", "out_made", "gated", "scale_made", "stats_in", "raw_made", "clamped", "turn_pool", "turn_sp", "inverted"))

    join_lag = 3 if layer == 1 else 0
    norm_lag = join_lag + 2
    work_lag = norm_lag
    after_lag = norm_lag + 1
    store_lag = work_lag + (6 if layer == 0 else 4)

    with nc.Block() as block:
        @block.sync
        def _(sp):
            def load(q):
                if not q.new:
                    sp.wait_ge(mixed_n if layer == 1 else joined, q.last)
                    sp.sem_inc(turn_sp, 1)
                sp.dma_start(place[q.h][:], k.places[bass.ds(q.H * ROWS, ROWS)].rearrange("(p g) -> p g", g=G)
                             ).then_inc(place_got[q.h], 16)
                if table_in is not None:
                    sp.dma_start(own_h[q.h][:], group_rows(table_in, q.H * ROWS)).then_inc(own_got[q.h], 16)

            def load_x(q):
                base, rows = q.H * ROWS, ROWS
                if x_in.shape[0] == k.N and isinstance(base, int):
                    rows = min(ROWS, k.N - base)
                    if rows <= 0:
                        base, rows = 0, ROWS
                if not q.new:
                    sp.wait_ge(joined if layer else normed, q.last)
                sp.dma_start(x[q.h][0:rows // G], group_rows(x_in, base, rows)).then_inc(x_got[q.h], 16)

            def store_x(q):
                base, rows = q.H * ROWS, ROWS
                if x_out.shape[0] == k.N and isinstance(base, int):
                    rows = max(0, min(ROWS, k.N - base))
                sp.wait_ge(joined, q.H + 1)
                if rows:
                    sp.dma_start(group_rows(x_out, base, rows), xc[q.h][0:rows // G]).then_inc(x_put[q.h], 16)

            def store_tables(q):
                if layer == 0:
                    sp.wait_ge(out_made, q.H + 1)
                    parts = [rows_h[q.h][:], pair_h[q.h][:]]
                else:
                    sp.wait_ge(out_made, G * (q.H + 1))
                    width = P + 8 if layer == 3 else D
                    parts = [out[q.h][:, :, n * width:(n + 1) * width] for n in range(n_put)]
                for table, part in zip(tables, parts):
                    sp.dma_start(group_rows(table, q.H * ROWS), part).then_inc(t_put[q.h], 16)

            sp.wait_ge(preset, S)
            stages = [(0, load), (join_lag // 2, load_x)] if agg is not None else [(0, load_x)]
            if x_out is not None:
                stages.append((4, store_x))
            if tables:
                stages.append((store_lag, store_tables))
            pipeline(sp, groups, stages, last_apart=True)
            for h in range(S):
                if n_put:
                    sp.wait_ge(t_put[h], 16 * n_put * uses_of(h, groups))
                if x_out is not None:
                    stored = uses_of(h, min(groups, -(-x_out.shape[0] // ROWS)))
                    sp.wait_ge(x_put[h], 16 * stored)

        @block.vector
        def _(dve):
            for h in range(S):
                nc.vector.memset(x[h][:], 0.0).then_inc(preset, 1)
            if not last_l:
                nc.vector.memset(minus_half[:], -0.5).then_inc(preset, 1)
            if layer == 1:
                nc.vector.memset(half[:], 0.5).then_inc(preset, 1)

            def mix(q):
                dve.wait_ge(own_got[q.h], 16 * (q.i + 1))
                dve.wait_ge(sums_got[q.h], 16 * G * (q.i + 1))
                if not q.new:
                    dve.wait_ge(joined, q.last)
                    dve.wait_ge(squared, G * q.last)
                steps = Steps(dve, joining, q.H, 2)
                steps(nc.vector.tensor_scalar(den[q.h][:, :, 0], sums[q.h][:, :, D], 1e-10, None, ALU.add))
                steps(nc.vector.reciprocal(inv[q.h][:, :, 0], den[q.h][:, :, 0]))
                steps.end()
                for g in range(G):
                    ins = nc.vector.scalar_tensor_tensor(mixed[q.h][:, g, :], sums[q.h][:, g, 0:D], inv[q.h][:, g, 0:1],
                                                         own_h[q.h][:, g, :], ALU.mult, ALU.add)
                ins.then_inc(mixed_n, 1)

            def join(q):
                dve.wait_ge(x_got[q.h], 16 * (q.i + 1))
                if layer == 0:
                    return
                if not q.new:
                    if layer == 1:
                        dve.wait_ge(product, G * q.last)
                    else:
                        dve.wait_ge(x_put[q.h], 16 * q.i)
                    if not last_l:
                        dve.wait_ge(normed, q.last)
                if layer == 1:
                    dve.wait_ge(factored, q.H + 1)
                    dve.wait_ge(mixed_n, q.H + 1)
                    for g in range(G):
                        ins = nc.vector.scalar_tensor_tensor(xc[q.h][:, g, :], mixed[q.h][:, g, :],
                                                             small[q.h][11][:, g:g + 1], x[q.h][:, g, :], ALU.mult, ALU.add)
                    ins.then_inc(joined, 1)
                elif layer in (2, 3):
                    dve.wait_ge(sums_got[q.h], 16 * G * (q.i + 1))
                    steps = Steps(dve, joining, q.H, 1)
                    steps(nc.vector.tensor_tensor(plain[q.h][:], x[q.h][:], sums[q.h][:, :, 0:D], ALU.add))
                    bias = (k.own_bias if layer == 2 else k.fc_bias)[:].rearrange("p (o f) -> p o f", o=1)
                    nc.vector.tensor_tensor(xc[q.h][:], plain[q.h][:], bias.to_broadcast([P, G, D]),
                                            ALU.add).then_inc(joined, 1)
                else:
                    dve.wait_ge(sums_got[q.h], 16 * G * (q.i + 1))
                    steps = Steps(dve, joining, q.H, 3)
                    heads = sums[q.h][:].rearrange("p g (n f) -> p (g n) f", n=4)
                    steps(nc.vector.tensor_scalar(den[q.h][:].rearrange("p g n -> p (g n)"), heads[:, :, 64], 1e-10, None, ALU.add))
                    steps(nc.vector.reciprocal(inv[q.h][:], den[q.h][:]))
                    steps(nc.vector.tensor_tensor(
                        scaled[q.h][:].rearrange("p g (n f) -> p (g n) f", n=4), heads[:, :, 0:64],
                        inv[q.h][:].rearrange("p g (n o) -> p (g n) o", o=1).to_broadcast([P, G * 4, 64]), ALU.mult))
                    nc.vector.tensor_tensor(xc[q.h][:], x[q.h][:], scaled[q.h][:], ALU.add).then_inc(joined, 1)
                if not last_l:
                    dve.wait_ge(joined, q.H + 1)

            def average(q):
                join(q)
                if last_l:
                    return
                if not q.new:
                    dve.wait_ge(normed, q.last)
                source = (xc if layer else x)[q.h]
                steps = Steps(dve, averaging, q.H, 2)
                for g in range(G):
                    ins = nc.vector.bn_stats(stats[q.h][:, g, :], source[:, g, :])
                steps(ins)
                dve.sem_inc(stats_in, 1)
                for g in range(G):
                    ins = nc.vector.bn_aggr(moments[q.h][:, g, :], stats[q.h][:, g, :])
                steps(ins)
                steps.end()
                nc.vector.tensor_scalar(var[q.h][:], moments[q.h][:, :, 1], 1e-5, None, ALU.add).then_inc(var_made, 1)

            def normalize(q):
                dve.wait_ge(std_made, q.H + 1)
                if not q.new:
                    dve.wait_ge(turned, G * q.last)
                source = (xc if layer else x)[q.h]
                for g in range(G):
                    ins = nc.vector.tensor_scalar(xn[q.h][:, g, :], source[:, g, :], moments[q.h][:, g, 0:1],
                                                  inv_std[q.h][:, g:g + 1], ALU.subtract, ALU.mult)
                ins.then_inc(normed, 1)

            def add_bias(q):
                if not q.new:
                    dve.wait_ge(out_made, q.last)
                for g in range(G):
                    dve.wait_ge(product, G * q.H + g + 1)
                    nc.vector.tensor_tensor(out[q.h][:, g, :], p_out[0][g][:, 0:n_out], k.bias0[:], ALU.add).then_inc(raw_made, 1)

            if last_l:
                pipeline(dve, groups, [(0, average)])
            elif layer == 1:
                pipeline(dve, groups, [(0, mix), (norm_lag, normalize), (join_lag, average)])
            elif layer == 0:
                pipeline(dve, groups, [(norm_lag, normalize), (0, average), (after_lag, add_bias)])
            else:
                pipeline(dve, groups, [(norm_lag, normalize), (0, average)])

        @block.gpsimd
        def _(pool):
            def scalar(*operands):
                pool.sem_inc(turn_pool, 1)
                return nc.gpsimd.tensor_scalar(*operands)

            def gather(q):
                pool.wait_ge(place_got[q.h], 16 * (q.i + 1))
                for g in range(G):
                    pool.sem_inc(turn_pool, 1)
                    nc.gpsimd.indirect_dma_start(sums[q.h][:, g, :], None, agg,
                                                 bass.IndirectOffsetOnAxis(place[q.h][:, g:g + 1], 0)).then_inc(sums_got[q.h], 16)

            def deviation(q):
                pool.wait_ge(var_made, q.H + 1)
                if not q.new:
                    pool.wait_ge(normed, q.last)
                nc.gpsimd.tensor_tensor(inv_std[q.h][:], var[q.h][:], minus_half[:], ALU.pow).then_inc(std_made, 1)

            def norm(q):
                s = small[q.h]
                pool.wait_ge(squared, G * (q.H + 1))
                if not q.new:
                    pool.wait_ge(joined, q.last)
                nc.gpsimd.tensor_tensor(s[4][:], s[2][:], half[:], ALU.pow).then_inc(clamped, 1)
                pool.wait_ge(clamped, 2 * q.H + 1)
                scalar(s[3][:], s[4][:], 1e-15, None, ALU.max).then_inc(clamped, 1)
                pool.wait_ge(clamped, 2 * q.H + 2)
                nc.gpsimd.tensor_tensor(s[5][:], s[3][:], k.minus_one[:], ALU.pow).then_inc(inverted, 1)

            def ball(q):
                s = small[q.h]
                steps = Steps(pool, pooling, q.H, 5)
                pool.wait_ge(inverted, q.H + 1)
                pool.wait_ge(tanhed, q.H + 1)
                steps(nc.gpsimd.tensor_tensor(s[7][:], s[6][:], s[5][:], ALU.mult))
                steps(nc.gpsimd.tensor_tensor(s[8][:], s[7][:], s[4][:], ALU.mult))
                scalar(s[0][:], s[8][:], 0.95, None, ALU.is_gt)
                steps(scalar(s[9][:], s[8][:], 1e-8, None, ALU.add))
                steps(nc.gpsimd.tensor_tensor(s[10][:], s[9][:], k.minus_one[:], ALU.pow))
                scalar(s[9][:], s[10][:], 0.95, -1.0, ALU.mult, ALU.add).then_inc(gated, 1)
                pool.wait_ge(gated, 2 * q.H + 1)
                nc.gpsimd.tensor_tensor(s[10][:], s[9][:], s[0][:], ALU.mult).then_inc(gated, 1)
                pool.wait_ge(gated, 2 * q.H + 2)
                steps(scalar(s[9][:], s[10][:], 1.0, None, ALU.add))
                steps.end()
                nc.gpsimd.tensor_tensor(s[11][:], s[9][:], s[7][:], ALU.mult).then_inc(factored, 1)

            def size(q):
                pool.wait_ge(gated, q.H + 1)
                steps = Steps(pool, pooling, q.H, 3)
                steps(scalar(size2m[q.h][:], size2[q.h][:], 1e-24, None, ALU.max))
                steps(nc.gpsimd.tensor_tensor(inv_size[q.h][:], size2m[q.h][:], minus_half[:], ALU.pow))
                steps(nc.gpsimd.tensor_tensor(size2m[q.h][:], inv_size[q.h][:], gate[q.h][:], ALU.mult))
                steps.end()
                if not q.new:
                    pool.wait_ge(out_made, q.last)
                scalar(scale[q.h][:], size2m[q.h][:], 1.5, None, ALU.mult).then_inc(scale_made, 1)

            if last_l:
                pipeline(pool, groups, [(0, gather)])
            else:
                pool.wait_ge(preset, S + (2 if layer == 1 else 1))
                pipeline(pool, groups, {
                    0: [(0, deviation), (after_lag, size)],
                    1: [(0, gather), (2 + GATHER_LAG, norm), (join_lag + 1 + GATHER_LAG, deviation), (2 + GATHER_LAG, ball)],
                }.get(layer, [(0, gather), (GATHER_LAG, deviation)]))

        @block.tensor
        def _(pe):
            def turn(q, g):
                t = G * q.H + g
                pe.wait_ge(normed, q.H + 1)
                if not (q.first and g < 2):
                    pe.wait_ge(rectified, t - 1)
                for c in range(2):
                    ins = nc.tensor.transpose(p_turn[g % 2][:, c * P:(c + 1) * P], xn[q.h][:, g, c * P:(c + 1) * P],
                                              k.ident[:])
                ins.then_inc(turned, 1)

            def work(q):
                if q.first:
                    turn(q, 0)
                for g in range(G):
                    t = G * q.H + g
                    if g + 1 < G:
                        turn(q, g + 1)
                    elif not q.final:
                        turn(q.next(), 0)
                    pe.wait_ge(rectified, t + 1)
                    if not (q.first and g < banks):
                        pe.wait_ge(raw_made if layer == 0 else out_made, t - banks + 1)
                    for w, (n, matrix) in enumerate(k.products[layer]):
                        for c in range(2):
                            ins = nc.tensor.matmul(p_out[w][g % banks][:, 0:n], h_t[g][:, c * P:(c + 1) * P], matrix[:, c, :],
                                                   start=c == 0, stop=c == 1 and layer != 1)
                    if layer == 1:
                        ins = nc.tensor.matmul(p_out[0][g % banks][:, D:2 * D], k.ident[:], xc[q.h][:, g, :],
                                               start=False, stop=True)
                    ins.then_inc(product, 1)
            if not last_l:
                pipeline(pe, groups, [(work_lag, work)], last_apart=True)

        @block.scalar
        def _(act):
            def squares(q):
                act.wait_ge(mixed_n, q.H + 1)
                for g in range(G):
                    if not (q.first and g < 2):
                        act.wait_ge(squared, G * q.H + g - 1)
                    nc.scalar.activation(junk[g % 2][:], mixed[q.h][:, g, :], ACT.Square,
                                         accum_out=small[q.h][2][:, g:g + 1]).then_inc(squared, 1)

            def bound(q):
                act.wait_ge(clamped, 2 * q.H + 2)
                nc.scalar.activation(small[q.h][6][:], small[q.h][3][:], ACT.Tanh).then_inc(tanhed, 1)

            def rectify(q, g):
                t = G * q.H + g
                act.wait_ge(turned, t + 1)
                if not q.first:
                    act.wait_ge(product, t - G + 1)
                nc.scalar.activation(h_t[g][:], p_turn[g % 2][:, 0:D], ACT.Relu).then_inc(rectified, 1)

            def work(q):
                if q.first:
                    rectify(q, 0)
                for g in range(G):
                    t = G * q.H + g
                    if g + 1 < G:
                        rectify(q, g + 1)
                    elif not q.final:
                        rectify(q.next(), 0)
                    if layer == 0:
                        continue
                    if not q.new and g == 0:
                        act.wait_ge(t_put[q.h], 16 * n_put * q.i)
                    act.wait_ge(product, t + 1)
                    if layer == 2:
                        nc.scalar.copy(out[q.h][:, g, 0:2 * D], p_out[0][g % banks][:])
                        nc.scalar.copy(out[q.h][:, g, 2 * D:3 * D], p_out[1][g % banks][:, 0:D]).then_inc(out_made, 1)
                    else:
                        nc.scalar.copy(out[q.h][:, g, :], p_out[0][g % banks][:, 0:n_out]).then_inc(out_made, 1)

            def measure(q):
                for g in range(G):
                    act.wait_ge(raw_made, G * q.H + g + 1)
                    if not (q.first and g < 2):
                        act.wait_ge(squared, G * q.H + g - 1)
                    nc.scalar.activation(junk[g % 2][:], out[q.h][:, g, 0:D], ACT.Square,
                                         accum_out=size2[q.h][:, g:g + 1]).then_inc(squared, 1)
                act.wait_ge(squared, G * (q.H + 1))
                nc.scalar.activation(gate[q.h][:], out[q.h][:, :, D], ACT.Sigmoid).then_inc(gated, 1)

            def resize(q):
                act.wait_ge(scale_made, q.H + 1)
                if not q.new:
                    act.wait_ge(t_put[q.h], 16 * n_put * q.i)
                for g in range(G):
                    nc.scalar.activation(rows_h[q.h][:, g, :], out[q.h][:, g, 0:D], ACT.Copy, scale=scale[q.h][:, g:g + 1])
                for g in range(G):
                    ins = nc.scalar.activation(pair_h[q.h][:, g, :], out[q.h][:, g, D + 1:D + 3], ACT.Copy,
                                               scale=scale[q.h][:, g:g + 1])
                ins.then_inc(out_made, 1)

            if not last_l:
                pipeline(act, groups, {
                    0: [(work_lag, work), (after_lag, measure), (after_lag + 1, resize)],
                    1: [(2, bound), (1, squares), (work_lag, work)],
                }.get(layer, [(work_lag, work)]), last_apart=True)
    ph.close()
def score_pass(nc, k, name, layer, table_src, table_dst=None, out=None, put=None, messages=None):
    ph = Phase(nc, name)
    NI, LAG = k.NT // U, 4
    W = {2: D, 3: 136}[layer]
    a = [ph.sb(f"a{j}", [P, W]) for j in range(U)]
    b = [ph.sb(f"b{j}", [P, W]) for j in range(U)] if table_dst is not None else None
    take_a, take_b, pos_i = (ph.sb(n, [P, U], I32) for n in ("take_a", "take_b", "pos_i"))
    z = [ph.sb(f"z{n}", [P, D]) for n in range(4)]
    score = ph.sb("score", [P, U, 2])
    indexed, turn_pool, scored, step = (ph.sem(n) for n in ("indexed", "turn_pool", "scored", "step"))
    got_a, got_b, put_s = (ph.sem_per_slot(n) for n in ("got_a", "got_b", "put"))
    each = {2: 2, 3: 3}[layer]

    with nc.Block() as block:
        @block.scalar
        def _(act):
            def index(t, j, late):
                if late is not None:
                    act.wait_ge(got_a[j], 16 * late)
                    if b is not None:
                        act.wait_ge(got_b[j], 16 * late)
                nc.scalar.copy(take_a[:, j:j + 1], columns(k.src_i, t)).then_inc(indexed, 1)
                if b is not None:
                    nc.scalar.copy(take_b[:, j:j + 1], columns(k.dst_i, t)).then_inc(indexed, 1)

            for j in range(LAG):
                index(j, j, None)

            def tiles(i, first):
                for j in range(U):
                    t = i * U + j
                    if j < U - LAG:
                        index(t + LAG, j + LAG, None if first else i)
                    else:
                        index(t + LAG, j + LAG - U, i + 1)
            peeled(act, NI, tiles)

        @block.gpsimd
        def _(pool):
            def store(t, j):
                pool.wait_ge(scored, t + 1)
                pool.sem_inc(turn_pool, 1)
                nc.gpsimd.indirect_dma_start(put, bass.IndirectOffsetOnAxis(pos_i[:, j:j + 1], 0), score[:, j, :],
                                             None, bounds_check=k.NP - 1, oob_is_err=False).then_inc(put_s[j], 16)

            def tiles(i, first):
                for j in range(U):
                    t = i * U + j
                    pool.wait_ge(indexed, (t + 1) * (1 if b is None else 2))
                    pool.sem_inc(turn_pool, 1)
                    if not first:
                        pool.wait_ge(scored, t - U + 1)
                        pool.sem_inc(turn_pool, 1)
                    nc.gpsimd.indirect_dma_start(a[j][:], None, table_src,
                                                 bass.IndirectOffsetOnAxis(take_a[:, j:j + 1], 0)).then_inc(got_a[j], 16)
                    if b is not None:
                        nc.gpsimd.indirect_dma_start(b[j][:], None, table_dst,
                                                     bass.IndirectOffsetOnAxis(take_b[:, j:j + 1], 0)).then_inc(got_b[j], 16)
                    if put is not None and (not first or j >= LAG):
                        store(t - LAG, (j - LAG) % U)
            peeled(pool, NI, tiles)
            if put is not None:
                for j in range(U - LAG, U):
                    store((NI - 1) * U + j, j)
                for j in range(U):
                    pool.wait_ge(put_s[j], 16 * NI)

        @block.vector
        def _(dve):
            def tiles(i, first):
                for j in range(U):
                    t = i * U + j
                    dve.wait_ge(got_a[j], 16 * (i + 1))
                    if b is not None:
                        dve.wait_ge(got_b[j], 16 * (i + 1))
                    s = Steps(dve, step, t, each)
                    z0, z1 = z[2 * (j % 2)], z[2 * (j % 2) + 1]
                    if layer == 2:
                        s(nc.vector.tensor_tensor(z0[:], a[j][:], b[j][:], ALU.add))
                        s(nc.vector.scalar_tensor_tensor(z1[:], z0[:], 0.2, z0[:], ALU.mult, ALU.max))
                        if not first:
                            dve.wait_ge(put_s[j], 16 * i)
                        nc.vector.tensor_copy(pos_i[:, j:j + 1], columns(k.pos_i, t))
                        nc.vector.tensor_copy(score[:, j, 1:2], k.fields[:, bass.ds(t, 1), 0])
                        nc.vector.tensor_tensor_reduce(z0[:], z1[:], k.attn[:], 1.0, 0.0, ALU.mult, ALU.add,
                                                       score[:, j, 0:1]).then_inc(scored, 1)
                    else:
                        fwd, rev = k.fields[:, bass.ds(t, 1), 3], k.fields[:, bass.ds(t, 1), 4]
                        nc.vector.tensor_scalar(z0[:, 0:64], a[j][:, 64:128], rev, None, ALU.mult)
                        s(nc.vector.tensor_scalar(z0[:, 64:68], a[j][:, 132:136], rev, None, ALU.mult))
                        nc.vector.scalar_tensor_tensor(messages[:, bass.ds(t, 1), 0:64].rearrange("p o f -> p (o f)"),
                                                       a[j][:, 0:64], fwd, z0[:, 0:64], ALU.mult, ALU.add)
                        s(nc.vector.scalar_tensor_tensor(z1[:, 0:4], a[j][:, 128:132], fwd, z0[:, 64:68], ALU.mult, ALU.add))
                        s(nc.vector.scalar_tensor_tensor(out[:, bass.ds(t, 1), :].rearrange("p o f -> p (o f)"),
                                                         z1[:, 0:4], 0.2, z1[:, 0:4], ALU.mult, ALU.max))
                        dve.sem_inc(scored, 1)
                    s.end()
            peeled(dve, NI, tiles)
    ph.close()


def to_rows(nc, k, name, cols, rows):
    ph = Phase(nc, name)
    p = ph.ps("p", [P, k.TC])
    turned, s_done = ph.sem("turned"), ph.sem("done")
    with nc.Block() as block:
        @block.tensor
        def _(pe):
            for b in range(k.TC // P):
                ins = nc.tensor.transpose(p[:, b * P:(b + 1) * P], cols[:, b * P:(b + 1) * P], k.ident[:])
            ins.then_inc(turned, 1)

        @block.vector
        def _(dve):
            dve.wait_ge(turned, 1)
            nc.vector.tensor_copy(rows[:].rearrange("p b q -> p (b q)"), p[:]).then_inc(s_done, 1)
    ph.close()


def powers(nc, k, name, rows, most, cols):
    ph = Phase(nc, name)
    less, power = ph.sb("less", [P, k.TC // P, P]), ph.sb("power", [P, k.TC // P, P])
    p = ph.ps("p", [P, k.TC])
    lessened, raised, turned, s_done = (ph.sem(n) for n in ("lessened", "raised", "turned", "done"))
    with nc.Block() as block:
        @block.vector
        def _(dve):
            nc.vector.tensor_tensor(less[:], rows[:], most[:], ALU.subtract).then_inc(lessened, 1)
            dve.wait_ge(turned, 1)
            nc.vector.tensor_copy(cols[:], p[:]).then_inc(s_done, 1)

        @block.scalar
        def _(act):
            act.wait_ge(lessened, 1)
            nc.scalar.activation(power[:], less[:], ACT.Exp).then_inc(raised, 1)

        @block.tensor
        def _(pe):
            pe.wait_ge(raised, 1)
            for b in range(k.TC // P):
                ins = nc.tensor.transpose(p[:, b * P:(b + 1) * P], power[:, b, :], k.ident[:])
            ins.then_inc(turned, 1)
    ph.close()


def shares_by_source(nc, k, scores, shares):
    hold = Phase(nc, "by_src")
    W = k.NT
    same_prev, same_next = hold.sb("same_prev", [P, 1, W]), hold.sb("same_next", [P, 1, W])
    whole = hold.sb("whole", [P, 1])
    score, most, power, total, share = (hold.sb(n, [P, 1, W]) for n in ("score", "most", "power", "total", "share"))
    inverse = hold.sb("inverse", [P, 1, W])
    segments(nc, k, "src_seg", scores, P, W, same_prev, same_next, whole, field=1)
    ph = Phase(nc, "src_in")
    pairs = ph.sb("pairs", [P, W, 2])
    landed, split = ph.sem("landed"), ph.sem("split")
    with nc.Block() as block:
        @block.sync
        def _(sp):
            sp.dma_start(pairs[:].rearrange("r w c -> r (w c)"), scores.rearrange("(r w) c -> r (w c)", w=W)).then_inc(landed, 16)

        @block.vector
        def _(dve):
            dve.wait_ge(landed, 16)
            nc.vector.tensor_copy(score[:, 0, :], pairs[:, :, 0]).then_inc(split, 1)
    ph.close()
    segment_reduce(nc, k, "src_max", score, same_prev, same_next, whole, "max", most)
    ph = Phase(nc, "src_exp")
    lessened, raised = ph.sem("lessened"), ph.sem("raised")
    with nc.Block() as block:
        @block.vector
        def _(dve):
            nc.vector.tensor_tensor(total[:], score[:], most[:], ALU.subtract).then_inc(lessened, 1)

        @block.scalar
        def _(act):
            act.wait_ge(lessened, 1)
            nc.scalar.activation(power[:], total[:], ACT.Exp).then_inc(raised, 1)
    ph.close()
    segment_reduce(nc, k, "src_sum", power, same_prev, same_next, whole, "sum", total)
    ph = Phase(nc, "src_out")
    step, stored = ph.sem("step"), ph.sem("stored")
    with nc.Block() as block:
        @block.vector
        def _(dve):
            chain = Chain(dve, step)
            chain(nc.vector.reciprocal(inverse[:], total[:]))
            chain(nc.vector.tensor_tensor(share[:], power[:], inverse[:], ALU.mult))

        @block.sync
        def _(sp):
            sp.wait_ge(step, 2)
            sp.dma_start(shares.rearrange("(r w) o -> r (w o)", w=W), share[:, 0, :]).then_inc(stored, 16)
            sp.wait_ge(stored, 16)
    ph.close()
    hold.close()


def head_powers(nc, k, scores, messages):
    ph = Phase(nc, "head_pow")
    NT = k.NT
    place_i, place = ph.sb("place_i", [P, NT], I32), ph.sb("place", [P, NT])
    far = ph.sb("far", [P, NT])
    most, all_most = ph.sb("most", [P, 4]), ph.sb("all_most", [P, 4])
    less = ph.sb("less", [P, NT, 4])
    counted, step, reduced, raised = (ph.sem(n) for n in ("counted", "step", "reduced", "raised"))
    with nc.Block() as block:
        @block.gpsimd
        def _(pool):
            nc.gpsimd.iota(place_i[:], pattern=[[P, NT]], base=0, channel_multiplier=1).then_inc(counted, 1)
            pool.wait_ge(step, 4)
            nc.gpsimd.partition_all_reduce(all_most[:], most[:], P, bass.bass_isa.ReduceOp.max).then_inc(reduced, 1)

        @block.vector
        def _(dve):
            chain = Chain(dve, step)
            dve.wait_ge(counted, 1)
            chain(nc.vector.tensor_copy(place[:], place_i[:]))
            chain(nc.vector.tensor_scalar(far[:], place[:], float(k.E), -FAR, ALU.is_ge, ALU.mult))
            chain(nc.vector.tensor_tensor(less[:], scores[:], far[:].rearrange("p (t o) -> p t o", o=1)
                                          .to_broadcast([P, NT, 4]), ALU.add))
            chain(nc.vector.tensor_reduce(most[:], less[:].rearrange("p t h -> p h t"), AX.X, ALU.max))
            dve.wait_ge(reduced, 1)
            chain(nc.vector.tensor_tensor(less[:], less[:], all_most[:].rearrange("p (o h) -> p o h", o=1)
                                          .to_broadcast([P, NT, 4]), ALU.subtract))
            chain(nc.vector.memset(messages[:, :, 64:65], 1.0))

        @block.scalar
        def _(act):
            act.wait_ge(step, 5)
            nc.scalar.activation(scores[:], less[:], ACT.Exp).then_inc(raised, 1)
    ph.close()


def weights(nc, k, a):
    ph = Phase(nc, "weights")
    square = [ph.sb(f"square{n}", [P, 2, D]) for n in range(4)]
    names = ["L0_gnn_W", "L2_gnn_W_s", "L2_gnn_W_t", "L2_gnn_W_fc"]
    flat = [ph.sb(f"flat{n}", [64, D]) for n in range(2)]
    attn0, bias0 = ph.sb("attn0", [P, 2, 2]), ph.sb("bias0", [P, 2])
    attn3 = ph.sb("attn3", [64, 4])
    bias_rows = ph.sb("bias_rows", [P, 2, P])
    spread_out = ph.sem("spread_out")
    p_turn = [ph.ps(f"p_turn{n}", [P, 512]) for n in range(4)]
    p_flat = ph.ps("p_flat", [P, 512])
    p_attn = ph.ps("p_attn", [P, 512])
    landed, turned, s_done = ph.sem("landed"), ph.sem("turned"), ph.sem("done")
    loads = [(square[n][:], a[name].rearrange("(d p) i -> p d i", p=P)) for n, name in enumerate(names)]
    loads += [(flat[0][:], a["L3_gnn_W_forward"]), (flat[1][:], a["L3_gnn_W_reverse"])]
    loads += [(k.w1[:, :, 0:D], a["L1_gnn_w_nbr"].rearrange("(c p) o -> p c o", p=P)),
              (k.w1[:, :, D:2 * D], a["L1_gnn_w_own"].rearrange("(c p) o -> p c o", p=P)),
              (k.own_bias[:], a["L1_gnn_bias"].rearrange("(o f) -> o f", o=1).to_broadcast([P, D])),
              (k.bias0[:, 0:D], a["L0_gnn_b"].rearrange("(o f) -> o f", o=1).to_broadcast([P, D])),
              (k.bias0[:, D:D + 1], a["L0_gnn_mag_b"].rearrange("(o f) -> o f", o=1).to_broadcast([P, 1])),
              (k.attn[:], a["L2_gnn_W_attn"].to_broadcast([P, D])),
              (k.fc_bias[:], a["L2_gnn_b_fc"].rearrange("(o f) -> o f", o=1).to_broadcast([P, D]))]
    thin = [(k.w0[:, c, D:D + 1], a["L0_gnn_mag_w"][:, c * P:(c + 1) * P].rearrange("o p -> p o")) for c in range(2)]
    thin += [(attn0[:, d, s:s + 1], a["L0_gnn_attn_w"][:, s * D + d * P:s * D + (d + 1) * P].rearrange("o p -> p o"))
             for d in range(2) for s in range(2)]
    thin += [(bias0[:, d:d + 1], a["L0_gnn_b"][d * P:(d + 1) * P].rearrange("(p o) -> p o", o=1)) for d in range(2)]
    thin += [(attn3[:, n:n + 1], a["L3_gnn_attn_forward"][0, n:n + 1, :].rearrange("o p -> p o")) for n in range(4)]
    with nc.Block() as block:
        @block.sync
        def _(sp):
            for to, frm in loads + thin:
                sp.dma_start(to, frm, allow_slow_non_contiguous=True).then_inc(landed, 16)

        @block.tensor
        def _(pe):
            pe.wait_ge(landed, 16 * len(loads + thin))
            for n in range(4):
                for c in range(2):
                    for d in range(2):
                        nc.tensor.transpose(p_turn[n][:, c * D + d * P:c * D + (d + 1) * P],
                                            square[n][:, d, c * P:(c + 1) * P], k.ident[:])
            for n in range(2):
                for c in range(2):
                    nc.tensor.transpose(p_flat[:, (c * 2 + n) * 64:(c * 2 + n) * 64 + 64], flat[n][:, c * P:(c + 1) * P],
                                        k.ident[0:64, 0:64])
            for c in range(2):
                for d in range(2):
                    nc.tensor.matmul(p_attn[:, 2 * c:2 * c + 2], square[0][:, d, c * P:(c + 1) * P], attn0[:, d, :],
                                     start=d == 0, stop=d == 1)
                for n in range(2):
                    nc.tensor.matmul(p_attn[:, 8 + (c * 2 + n) * 4:12 + (c * 2 + n) * 4], flat[n][:, c * P:(c + 1) * P],
                                     attn3[:], start=True, stop=True)
            pe.wait_ge(spread_out, 2)
            for d in range(2):
                ins = nc.tensor.matmul(p_attn[:, 4:6], bias_rows[:, d, :], attn0[:, d, :], start=d == 0, stop=d == 1)
            ins.then_inc(turned, 1)

        @block.vector
        def _(dve):
            nc.vector.memset(k.minus_one[:], -1.0).then_inc(s_done, 1)
            dve.wait_ge(landed, 16 * len(loads + thin))
            for d in range(2):
                nc.vector.tensor_scalar(bias_rows[:, d, :], k.ones[:], bias0[:, d:d + 1], None, ALU.mult).then_inc(spread_out, 1)
            dve.wait_ge(turned, 1)
            to = [k.w0[:, :, 0:D], k.w2[:, :, 0:D], k.w2[:, :, D:2 * D], k.w2[:, :, 2 * D:3 * D]]
            for n in range(4):
                nc.vector.tensor_copy(to[n], p_turn[n][:].rearrange("p (c o) -> p c o", c=2)).then_inc(s_done, 1)
            nc.vector.tensor_copy(k.w3[:, :, 0:P], p_flat[:, 0:2 * P].rearrange("p (c o) -> p c o", c=2)).then_inc(s_done, 1)
            nc.vector.tensor_copy(k.w0[:, :, D + 1:D + 3], p_attn[:, 0:4].rearrange("p (c o) -> p c o", c=2)).then_inc(s_done, 1)
            nc.vector.tensor_copy(k.w3[:, :, P:P + 8], p_attn[:, 8:24].rearrange("p (c o) -> p c o", c=2)).then_inc(s_done, 1)
            nc.vector.tensor_copy(k.bias0[:, D + 1:D + 3], p_attn[:, 4:6]).then_inc(s_done, 1)
    ph.close()


class Kept:
    pass


def gnn_kernel(nc, a, out, check=None):
    k = Kept()
    k.N, k.E = a["x"].shape[0], a["src"].shape[0]
    k.NT = -(-max(k.N, k.E) // (P * U)) * U
    k.NP = k.NT * P
    k.TC = -(-(k.NT + U) // P) * P
    B = k.TC // P
    assert k.N == k.E and k.N % G == 0

    def dram(name, shape):
        return nc.dram_tensor(name, shape, F32).ap()

    with ExitStack() as ctx:
        def sb(name, shape, dt=F32):
            return ctx.enter_context(nc.sbuf_tensor(name, shape, dt))

        k.ones, k.ident, k.before = sb("ones", [P, P]), sb("ident", [P, P]), sb("before", [P, P])
        k.unsorted = sb("unsorted", [1, 1], I32)
        k.ident_bf = sb("ident_bf", [P, P], BF16)
        k.ramp_i, k.ramp = sb("ramp_i", [P, k.TC], I32), sb("ramp", [P, k.TC])
        k.fields = sb("fields", [P, k.TC, 5])
        k.src_i, k.dst_i, k.pos_i = (sb(n, [P, k.TC], I32) for n in ("src_i", "dst_i", "pos_i"))
        k.dst_before = sb("dst_before", [P, k.TC])
        k.d_prev, k.d_next, k.d_whole = sb("d_prev", [P, B, P]), sb("d_next", [P, B, P]), sb("d_whole", [P, B])
        k.w0, k.w1 = sb("w0", [P, 2, D + 3]), sb("w1", [P, 2, 2 * D])
        k.w2, k.w3 = sb("w2", [P, 2, 3 * D]), sb("w3", [P, 2, P + 8])
        k.bias0, k.own_bias, k.minus_one = sb("bias0", [P, D + 3]), sb("own_bias", [P, D]), sb("minus_one", [P, G])
        k.attn, k.fc_bias = sb("attn", [P, D]), sb("fc_bias", [P, D])
        k.dst_f = lambda t: k.fields[:, bass.ds(t, 1), 1]
        k.products = {0: [(D + 3, k.w0)], 1: [(2 * D, k.w1)],
                      2: [(2 * D, k.w2[:, :, 0:2 * D]), (D, k.w2[:, :, 2 * D:3 * D])], 3: [(P + 8, k.w3)], 4: []}

        sorted_rows, k.dst_keys = dram("sorted_rows", (k.NP, 5)), dram("dst_keys", (k.NP,))
        scores, shares = dram("scores", (k.NP, 2)), dram("shares", (k.NP, 1))
        agg = dram("agg", (k.NP + 1, AGG_W))
        k.places = nc.dram_tensor("places", (k.NP,), I32).ap()
        h0, ends0 = dram("h0", (k.NP, D)), dram("ends0", (k.NP, 2))
        h1, from_src, to_dst, h2, h3 = (dram(n, (k.NP, w)) for n, w in
                                        (("h1", D), ("from_src", D), ("to_dst", D), ("h2", D), ("h3", P + 8)))
        x1, x2, x3 = (dram(n, (k.NP, D)) for n in ("x1", "x2", "x3"))

        constants(nc, k)
        weights(nc, k, a)
        load_edges(nc, k, a, sorted_rows)
        rank_phase(nc, k, "by_dst", k.fields[:, :, 1],
                   lambda t: k.fields[:, bass.ds(t, 1), :].rearrange("p o f -> p (o f)"), 5, sorted_rows,
                   only_if=k.unsorted)
        sorted_edges(nc, k, sorted_rows, k.dst_keys)
        segments(nc, k, "dst_seg", k.dst_keys.rearrange("(r c) -> r c", c=1), k.NT, P, k.d_prev, k.d_next, k.d_whole)
        edge_columns(nc, k)
        last_places(nc, k, agg, k.places)
        node_pass(nc, k, 0, a["x"], tables=(h0, ends0))
        hold = Phase(nc, "soft0")
        score, power = hold.sb("score", [P, k.TC]), hold.sb("power", [P, k.TC])
        rows, most = hold.sb("rows", [P, B, P]), hold.sb("most", [P, B, P])
        zero = hold.sem("zero")
        with nc.Block() as block:
            @block.vector
            def _(dve):
                nc.vector.memset(score[:], 0.0).then_inc(zero, 1)
        rank_phase(nc, k, "rank_src", k.fields[:, :, 0], pos_out=k.pos_i, beside=EndSums(nc, k, ends0, score))
        to_rows(nc, k, "rows0", score, rows)
        segment_reduce(nc, k, "max0", rows, k.d_prev, k.d_next, k.d_whole, "max", most)
        powers(nc, k, "pow0", rows, most, power)
        aggregate(nc, k, "agg0", agg, table=h0, weight=lambda t: columns(power, t), ones=True)
        hold.close()

        node_pass(nc, k, 1, a["x"], agg=agg, table_in=h0, tables=(h1, x1))
        aggregate(nc, k, "agg1", agg, table=h1, weight=lambda t: k.fields[:, bass.ds(t, 1), 2])

        node_pass(nc, k, 2, x1, x_out=x2, agg=agg, tables=(from_src, to_dst, h2))
        score_pass(nc, k, "score2", 2, from_src, to_dst, put=scores)
        shares_by_source(nc, k, scores, shares)
        aggregate(nc, k, "agg2", agg, table=h2, alpha=shares)

        node_pass(nc, k, 3, x2, x_out=x3, agg=agg, tables=(h3,))
        hold = Phase(nc, "soft3")
        messages, head_scores = hold.sb("messages", [P, k.NT, 65]), hold.sb("head_scores", [P, k.NT, 4])
        score_pass(nc, k, "score3", 3, h3, out=head_scores, messages=messages)
        head_powers(nc, k, head_scores, messages)
        aggregate(nc, k, "agg3", agg, heads=(
            lambda t: messages[:, bass.ds(t, 1), :].rearrange("p o f -> p (o f)"),
            lambda t: head_scores[:, bass.ds(t, 1), :].rearrange("p o f -> p (o f)")))
        hold.close()
        node_pass(nc, k, 4, x3, x_out=out, agg=agg)


_INS = ["x", "src", "dst", "edge_attr_2", "edge_weight", "L0_gnn_W", "L0_gnn_b", "L0_gnn_mag_w", "L0_gnn_mag_b",
        "L0_gnn_attn_w", "L1_gnn_w_nbr", "L1_gnn_w_own", "L1_gnn_bias", "L2_gnn_W_s", "L2_gnn_W_t", "L2_gnn_W_attn",
        "L2_gnn_W_fc", "L2_gnn_b_fc", "L3_gnn_W_forward", "L3_gnn_W_reverse", "L3_gnn_attn_forward"]


def kernel(**inputs):
    import numpy as np
    import concourse.bacc as bacc
    from concourse.bass_utils import run_bass_kernel_spmd

    nc = bacc.Bacc("TRN2", target_bir_lowering=False, num_devices=1)
    arrays, aps = {}, {}
    for name in _INS:
        array = np.ascontiguousarray(inputs[name])
        arrays[f"in_{name}"] = array
        aps[name] = nc.dram_tensor(f"in_{name}", array.shape, mybir.dt.from_np(array.dtype), kind="ExternalInput").ap()
    out = nc.dram_tensor("out_0", arrays["in_x"].shape, F32, kind="ExternalOutput").ap()
    gnn_kernel(nc, aps, out)
    result = run_bass_kernel_spmd(nc, [arrays], core_ids=[0])
    return result.results[0]["out_0"]
```
